# Optimizing a Trainium2 kernel written in Bass

```python
import numpy as np
import jax
import jax.numpy as jnp

def _softmax(x, axis=-1):
    return jax.nn.softmax(x, axis=axis)

def _gelu(x):
    return jax.nn.gelu(x, approximate=True)

def _silu(x):
    return jax.nn.silu(x)

def _sigmoid(x):
    return jax.nn.sigmoid(x)

def _layernorm(x, axis=-1, eps=1e-05):
    m = jnp.mean(x, axis=axis, keepdims=True)
    v = jnp.var(x, axis=axis, keepdims=True)
    return (x - m) / jnp.sqrt(v + eps)

def _scatter_add(tgt, idx, src, axis=0):
    return tgt.at[idx].add(src)

def _segment_sum(src, seg, n):
    return jax.ops.segment_sum(src, seg, n)
kernel_name = 'mk_gnn_resnorm_d4_gnn_r8_036b85'

def setup_inputs(seed: int=0):
    np.random.seed(seed)
    _w = jnp.asarray

    def _rec_inputs():
        import jax
        import jax.numpy as jnp
        _gk = jax.random.key(seed)
        x = -0.000202 + 1 * jax.random.normal(jax.random.fold_in(_gk, 1), (12500, 128), jnp.float32)
        src = jax.random.randint(jax.random.fold_in(_gk, 2), (200000,), 0, 12500, jnp.int32)
        dst = jax.random.randint(jax.random.fold_in(_gk, 3), (200000,), 0, 12500, jnp.int32)
        _o = jnp.argsort(dst, stable=True)
        src = src[_o]
        dst = dst[_o]
        edge_type_32 = jax.random.randint(jax.random.fold_in(_gk, 13), (200000,), 0, 32, jnp.int32)
        edge_type_8 = jax.random.randint(jax.random.fold_in(_gk, 14), (200000,), 0, 8, jnp.int32)
        return (x, src, dst, edge_type_32, edge_type_8)
    x, src, dst, edge_type_32, edge_type_8 = _rec_inputs()

    def _L0_gnn_setup():
        import jax, jax.numpy as jnp
        import numpy as np
        N_NODES = 6250
        N_EDGES = 100000
        IN_FEAT = 128
        OUT_FEAT = 128
        NUM_RELS = 8
        key = jax.random.key(seed)
        k_h, k_w, k_b, k_s, k_d, k_r = jax.random.split(key, 6)
        return {'h': jax.random.normal(k_h, (N_NODES, IN_FEAT), dtype=jnp.float32), 'weight': jax.random.normal(k_w, (NUM_RELS + 1, IN_FEAT, OUT_FEAT), dtype=jnp.float32) * (1.0 / np.sqrt(IN_FEAT)), 'bias': jax.random.normal(k_b, (NUM_RELS + 1, OUT_FEAT), dtype=jnp.float32) * 0.02, 'src': jax.random.randint(k_s, (N_EDGES,), 0, N_NODES, dtype=jnp.int32), 'dst': jax.random.randint(k_d, (N_EDGES,), 0, N_NODES, dtype=jnp.int32), 'rel': jax.random.randint(k_r, (N_EDGES,), 0, NUM_RELS, dtype=jnp.int32)}
    _L0_gnn_all = _L0_gnn_setup()
    _L0_gnn_in = {k: v for k, v in _L0_gnn_all.items() if k in ('weight', 'bias')}
    del _L0_gnn_all

    def _L1_gnn_setup():
        import jax, jax.numpy as jnp
        import numpy as np
        N_NODES = 6250
        N_EDGES = 78125
        D_IN = 128
        D_OUT = 128
        key = jax.random.key(seed)
        k1, k2, k3, k4 = jax.random.split(key, 4)
        x = jax.random.normal(k1, (N_NODES, D_IN), dtype=jnp.float32)
        edge_index = jax.random.randint(k2, (2, N_EDGES), 0, N_NODES, dtype=jnp.int64)
        bound = 1.0 / np.sqrt(D_IN)
        W = jax.random.uniform(k3, (D_OUT, D_IN), dtype=jnp.float32, minval=-bound, maxval=bound)
        b = jax.random.uniform(k4, (D_OUT,), dtype=jnp.float32, minval=-bound, maxval=bound)
        return {'x': x, 'edge_index': edge_index, 'W': W, 'b': b}
    _L1_gnn_all = _L1_gnn_setup()
    _L1_gnn_in = {k: v for k, v in _L1_gnn_all.items() if k in ('W', 'b')}
    del _L1_gnn_all

    def _L2_gnn_setup():
        import jax, jax.numpy as jnp
        import numpy as np
        N_NODES = 6250
        N_EDGES = 200000
        IN_FEATS = 128
        HID = 128
        HEADS = 4
        F_HEAD = HID // HEADS
        NEG_SLOPE = 0.2
        key = jax.random.key(seed)
        ks = jax.random.split(key, 7)
        feat = jax.random.normal(ks[0], (N_NODES, IN_FEATS), dtype=jnp.float32)
        W = jax.random.normal(ks[1], (IN_FEATS, HID), dtype=jnp.float32) * (1.0 / np.sqrt(IN_FEATS))
        attn_l = jax.random.normal(ks[2], (HEADS, F_HEAD), dtype=jnp.float32) * 0.1
        attn_r = jax.random.normal(ks[3], (HEADS, F_HEAD), dtype=jnp.float32) * 0.1
        bias = jnp.zeros((HID,), dtype=jnp.float32)
        src_idx = jax.random.randint(ks[4], (N_EDGES,), 0, N_NODES, dtype=jnp.int32)
        dst_idx = jax.random.randint(ks[5], (N_EDGES,), 0, N_NODES, dtype=jnp.int32)
        return {'feat': feat, 'W': W, 'attn_l': attn_l, 'attn_r': attn_r, 'bias': bias, 'src_idx': src_idx, 'dst_idx': dst_idx}
    _L2_gnn_all = _L2_gnn_setup()
    _L2_gnn_in = {k: v for k, v in _L2_gnn_all.items() if k in ('W', 'attn_l', 'attn_r', 'bias')}
    del _L2_gnn_all

    def _L3_gnn_setup():
        import jax, jax.numpy as jnp
        import numpy as np
        N = 3750
        E = 120000
        DIN = 128
        DOUT = 128
        R = 32
        NUM_RULES = 100
        ACTIVE = 4
        EPS = 1e-05
        key = jax.random.key(seed)
        ks = jax.random.split(key, 10)
        x = jax.random.normal(ks[0], (N, DIN), jnp.float32)
        src = jax.random.randint(ks[1], (E,), 0, N)
        dst = jax.random.randint(ks[2], (E,), 0, N)
        edge_type = jax.random.randint(ks[3], (E,), 0, R)
        rule_ids = jax.random.randint(ks[4], (ACTIVE,), 0, NUM_RULES)
        W_r = jax.random.normal(ks[5], (R, DIN, DOUT), jnp.float32) * 0.05
        Wq_w = jax.random.normal(ks[6], (DIN, DOUT), jnp.float32) * 0.05
        Wq_b = jnp.zeros((DOUT,), jnp.float32)
        Wk_w = jax.random.normal(ks[7], (3 * DIN, DOUT), jnp.float32) * 0.05
        Wk_b = jnp.zeros((DOUT,), jnp.float32)
        rule_emb = jax.random.normal(ks[8], (NUM_RULES, DIN), jnp.float32) * 0.05
        bias = jnp.zeros((DOUT,), jnp.float32)
        ln_gamma = jnp.ones((DOUT,), jnp.float32)
        ln_beta = jnp.zeros((DOUT,), jnp.float32)
        return {'x': x, 'W_r': W_r, 'Wq_w': Wq_w, 'Wq_b': Wq_b, 'Wk_w': Wk_w, 'Wk_b': Wk_b, 'rule_emb': rule_emb, 'bias': bias, 'ln_gamma': ln_gamma, 'ln_beta': ln_beta, 'src': src, 'dst': dst, 'edge_type': edge_type, 'rule_ids': rule_ids}
    _L3_gnn_all = _L3_gnn_setup()
    _L3_gnn_in = {k: v for k, v in _L3_gnn_all.items() if k in ('W_r', 'Wq_w', 'Wq_b', 'Wk_w', 'Wk_b', 'rule_emb', 'bias', 'ln_gamma', 'ln_beta', 'rule_ids')}
    del _L3_gnn_all
    return {'x': x, 'src': src, 'dst': dst, 'edge_type_32': edge_type_32, 'edge_type_8': edge_type_8, 'L0_gnn_weight': _L0_gnn_in['weight'], 'L0_gnn_bias': _L0_gnn_in['bias'], 'L1_gnn_W': _L1_gnn_in['W'], 'L1_gnn_b': _L1_gnn_in['b'], 'L2_gnn_W': _L2_gnn_in['W'], 'L2_gnn_attn_l': _L2_gnn_in['attn_l'], 'L2_gnn_attn_r': _L2_gnn_in['attn_r'], 'L2_gnn_bias': _L2_gnn_in['bias'], 'L3_gnn_W_r': _L3_gnn_in['W_r'], 'L3_gnn_Wq_w': _L3_gnn_in['Wq_w'], 'L3_gnn_Wq_b': _L3_gnn_in['Wq_b'], 'L3_gnn_Wk_w': _L3_gnn_in['Wk_w'], 'L3_gnn_Wk_b': _L3_gnn_in['Wk_b'], 'L3_gnn_rule_emb': _L3_gnn_in['rule_emb'], 'L3_gnn_bias': _L3_gnn_in['bias'], 'L3_gnn_ln_gamma': _L3_gnn_in['ln_gamma'], 'L3_gnn_ln_beta': _L3_gnn_in['ln_beta'], 'L3_gnn_rule_ids': _L3_gnn_in['rule_ids']}

def reference(x, src, dst, edge_type_32, edge_type_8, L0_gnn_weight, L0_gnn_bias, L1_gnn_W, L1_gnn_b, L2_gnn_W, L2_gnn_attn_l, L2_gnn_attn_r, L2_gnn_bias, L3_gnn_W_r, L3_gnn_Wq_w, L3_gnn_Wq_b, L3_gnn_Wk_w, L3_gnn_Wk_b, L3_gnn_rule_emb, L3_gnn_bias, L3_gnn_ln_gamma, L3_gnn_ln_beta, L3_gnn_rule_ids):
    import jax
    import jax.numpy as jnp

    def _L0_gnn_ref(h, weight, bias, src, dst, rel):
        import jax, jax.numpy as jnp
        import numpy as np
        N_NODES = 6250
        N_EDGES = 100000
        IN_FEAT = 128
        OUT_FEAT = 128
        NUM_RELS = 8
        n = h.shape[0]
        hw = jnp.einsum('ni,rio->rno', h, weight)
        msg = hw[rel, src] + bias[rel]
        agg = jax.ops.segment_max(msg, dst, num_segments=n)
        in_deg = jax.ops.segment_sum(jnp.ones((msg.shape[0],), dtype=jnp.int32), dst, num_segments=n)
        agg = jnp.where((in_deg > 0)[:, None], agg, 0.0)
        out = hw[-1] + agg + bias[-1]
        return jax.nn.relu(out)

    def _L1_gnn_ref(x, edge_index, W, b):
        import jax, jax.numpy as jnp
        import numpy as np
        N_NODES = 6250
        N_EDGES = 78125
        D_IN = 128
        D_OUT = 128
        num_nodes = x.shape[0]
        h = x @ W.T + b
        in_node, out_node = (edge_index[0], edge_index[1])
        msgs = h[in_node]
        sums = jax.ops.segment_sum(msgs, out_node, num_segments=num_nodes)
        ones = jnp.ones((edge_index.shape[1],), dtype=h.dtype)
        counts = jax.ops.segment_sum(ones, out_node, num_segments=num_nodes)
        mean = sums / jnp.maximum(counts, 1.0)[:, None]
        return jax.nn.relu(mean)

    def _L2_gnn_ref(feat, W, attn_l, attn_r, bias, src_idx, dst_idx):
        import jax, jax.numpy as jnp
        import numpy as np
        N_NODES = 6250
        N_EDGES = 200000
        IN_FEATS = 128
        HID = 128
        HEADS = 4
        F_HEAD = HID // HEADS
        NEG_SLOPE = 0.2
        N = feat.shape[0]
        ft = (feat @ W).reshape(N, HEADS, F_HEAD)
        el = jnp.einsum('nhf,hf->nh', ft, attn_l)
        er = jnp.einsum('nhf,hf->nh', ft, attn_r)
        e = jax.nn.leaky_relu(el[src_idx] + er[dst_idx], negative_slope=NEG_SLOPE)
        m = jax.ops.segment_max(e, dst_idx, num_segments=N)
        m = jnp.where(jnp.isfinite(m), m, 0.0)
        a = jnp.exp(e - m[dst_idx])
        s = jax.ops.segment_sum(a, dst_idx, num_segments=N)
        alpha = a / jnp.where(s[dst_idx] > 0, s[dst_idx], 1.0)
        msgs = ft[src_idx] * alpha[:, :, None]
        out = jax.ops.segment_sum(msgs, dst_idx, num_segments=N)
        out = out + bias.reshape(1, HEADS, F_HEAD)
        return out.reshape(N, HEADS * F_HEAD)

    def _L3_gnn_ref(x, W_r, Wq_w, Wq_b, Wk_w, Wk_b, rule_emb, bias, ln_gamma, ln_beta, src, dst, edge_type, rule_ids):
        import jax, jax.numpy as jnp
        import numpy as np
        N = 3750
        E = 120000
        DIN = 128
        DOUT = 128
        R = 32
        NUM_RULES = 100
        ACTIVE = 4
        EPS = 1e-05
        n_nodes, _ = x.shape
        n_rel, _, dout = W_r.shape
        scale = 1.0 / jnp.sqrt(jnp.float32(dout))
        h_R = rule_emb[rule_ids]
        q = (x @ Wq_w + Wq_b)[dst]
        Wk1, Wk2, Wk3 = jnp.split(Wk_w, 3, axis=0)
        h_rel = W_r.mean(axis=-1)
        k_node = x @ Wk1
        k_rel = h_rel @ Wk2
        v_rule = h_R @ Wk3
        k_base = k_node[src] + k_rel[edge_type] + Wk_b
        score_base = jnp.sum(q * k_base, axis=-1)
        scores = (score_base[:, None] + q @ v_rule.T) * scale
        seg = edge_type * n_nodes + dst
        nseg = n_rel * n_nodes
        m = jax.ops.segment_max(scores, seg, num_segments=nseg)
        ex = jnp.exp(scores - m[seg])
        s = jax.ops.segment_sum(ex, seg, num_segments=nseg)
        attn = ex / s[seg]
        attn_mean = attn.mean(axis=-1)
        proj = jnp.einsum('nd,rdo->nro', x, W_r)
        msg = proj[src, edge_type] * attn_mean[:, None]
        out = jax.ops.segment_sum(msg, dst, num_segments=n_nodes) + bias
        mu = out.mean(axis=-1, keepdims=True)
        var = out.var(axis=-1, keepdims=True)
        out = (out - mu) * jax.lax.rsqrt(var + EPS) * ln_gamma + ln_beta
        return jax.nn.relu(out)
    edge_index = jnp.stack([src, dst])
    x = _layernorm(x + _L0_gnn_ref(x, L0_gnn_weight, L0_gnn_bias, src, dst, edge_type_8), axis=-1)
    x = _layernorm(x + _L1_gnn_ref(x, edge_index, L1_gnn_W, L1_gnn_b), axis=-1)
    x = _layernorm(x + _L2_gnn_ref(x, L2_gnn_W, L2_gnn_attn_l, L2_gnn_attn_r, L2_gnn_bias, src, dst), axis=-1)
    x = _layernorm(x + _L3_gnn_ref(x, L3_gnn_W_r, L3_gnn_Wq_w, L3_gnn_Wq_b, L3_gnn_Wk_w, L3_gnn_Wk_b, L3_gnn_rule_emb, L3_gnn_bias, L3_gnn_ln_gamma, L3_gnn_ln_beta, src, dst, edge_type_32, L3_gnn_rule_ids), axis=-1)
    return x

_drawn_inputs = setup_inputs


def setup_inputs(seed=0):
    import zlib

    import numpy as np

    out = dict(_drawn_inputs(seed))
    spreads = {'L2_gnn_bias': (0.0, 0.1),
     'L3_gnn_Wq_b': (0.0, 0.8),
     'L3_gnn_Wk_b': (0.0, 0.8),
     'L3_gnn_bias': (0.0, 0.1),
     'L3_gnn_ln_gamma': (1.0, 0.2),
     'L3_gnn_ln_beta': (0.0, 0.1)}
    factors = {'L3_gnn_rule_emb': 8.0}
    for name, (base, spread) in spreads.items():
        noise = np.random.default_rng([zlib.crc32(name.encode()), seed]).standard_normal(out[name].shape)
        drawn = base * np.exp(spread * noise) if base else spread * noise
        out[name] = jnp.asarray(drawn.astype(out[name].dtype))
    for name, factor in factors.items():
        out[name] = (out[name] * factor).astype(out[name].dtype)
    return out
```

```python
from contextlib import ExitStack

import concourse.bass as bass
from concourse import mybir

ALU = mybir.AluOpType
ACT = mybir.ActivationFunctionType
F32 = mybir.dt.float32
BF16 = mybir.dt.bfloat16
I32 = mybir.dt.int32

P = 128
T = 4
B = T * P
RING = 4
HEADS = 4
RELS = 32
RELS0 = 8
HUGE = 3e38
MASKED = -1e28
EPS = 1e-5
SLOPE = 0.2
CREDIT = 4


class Step:

    def __init__(self, i, k, ring):
        self.n, self.k, self.turn = i * ring + k, k % ring, i + k // ring
        self.prev = (k - 1) % ring


def done(s, back=0):
    return s.n + (CREDIT + 1 - back)


def run(eng, count, ring, stages):
    turns = count // ring

    def edge(steps):
        for m in steps:
            for stage, offset in stages:
                if 0 <= m + offset < count:
                    stage(Step(0, m + offset, ring))

    first = 1 + (min(offset for _, offset in stages) < 0)
    edge(range(-max(offset for _, offset in stages), first * ring))
    with eng.Fori(first, turns - 1) as i:
        for k in range(ring):
            for stage, offset in stages:
                stage(Step(i, k + offset, ring))
    edge(range(ring * (turns - 1), count - min(offset for _, offset in stages)))


class Kernel:
    def __init__(self, nc, io, n_nodes, n_edges):
        self.nc, self.io = nc, io
        self.NTN = n_nodes // P
        self.NT = n_edges // P
        self.NB = n_edges // B
        self.NP, self.EP = n_nodes, n_edges
        self.ctx = ExitStack()
        self.sems = []

    def sem(self, ctx, name):
        self.sems.append(self.nc.alloc_semaphore(name))
        return self.sems[-1]

    def phase(self, ctx):
        nc = self.nc

        def clear():
            nc.all_engine_barrier()
            nc.clear_and_free_semaphores(self.sems)
            nc.all_engine_barrier()
            self.sems = []

        ctx.callback(clear)
        return ctx.enter_context(nc.Block())

    def sb(self, ctx, name, shape, dt=F32):
        return ctx.enter_context(self.nc.sbuf_tensor(name, shape, dt))

    def bank(self, ctx, name, shape=(P, B), dt=F32):
        return ctx.enter_context(self.nc.psum_tensor(name, list(shape), dt))

    def dram(self, name, shape, dt=F32):
        return self.nc.dram_tensor(name, shape, dt, kind="Internal").ap()


def make_constants(K):
    nc, io, sb = K.nc, K.io, K.sb
    c = K.ctx
    K.ident = sb(c, "ident", [P, P])
    K.ones = sb(c, "ones", [P, P])
    K.quarter = sb(c, "quarter", [P, P])
    K.upper = sb(c, "upper", [P, P])
    K.w0 = sb(c, "w0", [P, (RELS0 + 1) * P])
    K.b0 = sb(c, "b0", [P, (RELS0 + 1) * P])
    K.w1t = sb(c, "w1t", [P, P])
    K.b1 = sb(c, "b1", [P, P])
    K.w2 = sb(c, "w2", [P, 2 * P])
    K.left = sb(c, "left", [P, P])
    K.b2 = sb(c, "b2", [P, P])
    K.wr = sb(c, "wr", [P, RELS * P])
    K.wkq = sb(c, "wkq", [P, 2 * P])
    K.bq = sb(c, "bq", [P, P])
    K.krel = sb(c, "krel", [RELS, P])
    K.rules = sb(c, "rules", [P, P])
    K.other = sb(c, "other", [RELS, P])
    K.relid = sb(c, "relid", [RELS, 1])
    K.b3 = sb(c, "b3", [P, P])
    K.gamma = sb(c, "gamma", [P, P])
    K.beta = sb(c, "beta", [P, P])
    K.eps = sb(c, "eps", [P, 1])
    K.first_rows = K.dram("first_rows", (K.EP + K.NP, P))

    with ExitStack() as t:
        zeros = sb(t, "zeros", [P, 4096])
        relid_i = sb(t, "relid_i", [RELS, 1], I32)
        right = sb(t, "right", [P, P])
        heads = sb(t, "heads", [P, P])
        al = sb(t, "al", [P, 1])
        ar = sb(t, "ar", [P, 1])
        w1 = sb(t, "w1", [P, P])
        w2t = sb(t, "w2t", [P, P])
        wk2 = sb(t, "wk2", [P, P])
        wk3 = sb(t, "wk3", [P, P])
        wkb = sb(t, "wkb", [RELS, P])
        hrel = sb(t, "hrel", [P, RELS])
        hrelm = sb(t, "hrelm", [P, RELS])
        ids = sb(t, "ids", [HEADS, 1], I32)
        emb = sb(t, "emb", [HEADS, P])
        embt = sb(t, "embt", [P, HEADS])
        vrule = sb(t, "vrule", [P, HEADS])
        pw1, pw2, pw2r = K.bank(t, "pw1"), K.bank(t, "pw2"), K.bank(t, "pw2r")
        pemb, pv, pk = K.bank(t, "pemb"), K.bank(t, "pv"), K.bank(t, "pk")
        loaded, zeroed, ids_in, emb_in = (K.sem(t, n) for n in ("c_loaded", "c_zeroed", "c_ids", "c_emb"))
        cleared, made, turned, copied = (K.sem(t, n) for n in ("c_cleared", "c_made", "c_turned", "c_copied"))
        products, chain, masks = K.sem(t, "c_products"), K.sem(t, "c_chain"), K.sem(t, "c_masks")
        LOADS = 18
        FILLS = (K.EP + K.NP) * P // (P * 4096)
        REST = (K.EP + K.NP) - FILLS * 4096
        block = K.phase(t)

        @block.sync
        def _(sp):
            def load(dst, src):
                sp.dma_start(dst, src).then_inc(loaded, 16)

            load(K.w0[:, :].rearrange("i (r o) -> i r o", o=P), io["w0"].rearrange("r i o -> i r o"))
            load(K.b0[:, :], io["b0"].rearrange("r o -> (r o)").partition_broadcast(P))
            load(w1[:, :], io["w1"])
            load(K.b1[:, :], io["b1"].partition_broadcast(P))
            load(K.w2[:, 0:P], io["w2"])
            load(al[:, :], io["attn_l"].rearrange("h (f a) -> (h f) a", a=1))
            load(ar[:, :], io["attn_r"].rearrange("h (f a) -> (h f) a", a=1))
            load(K.b2[:, :], io["b2"].partition_broadcast(P))
            load(K.wr[:, :].rearrange("i (r o) -> i r o", o=P), io["wr"].rearrange("r i o -> i r o"))
            load(K.wkq[:, 0:P], io["wk"][0:P, :])
            load(K.wkq[:, P:2 * P], io["wq"])
            load(wk2[:, :], io["wk"][P:2 * P, :])
            load(wk3[:, :], io["wk"][2 * P:3 * P, :])
            load(K.bq[:, :], io["bq"].partition_broadcast(P))
            load(wkb[:, :], io["bk"].partition_broadcast(RELS))
            load(K.b3[:, :], io["b3"].partition_broadcast(P))
            load(K.gamma[:, :], io["gamma"].partition_broadcast(P))
            load(K.beta[:, :], io["beta"].partition_broadcast(P))
            sp.dma_start(ids[:, :], io["rule_ids"].rearrange("(k a) -> k a", a=1)).then_inc(ids_in, 16)
            sp.wait_ge(cleared, 1)
            flat = K.first_rows.rearrange("e f -> (e f)")
            for n in range(FILLS):
                sp.dma_start(flat[n * P * 4096:(n + 1) * P * 4096].rearrange("(p x) -> p x", p=P),
                             zeros[:, :]).then_inc(zeroed, 16)
            if REST:
                sp.dma_start(flat[FILLS * P * 4096:].rearrange("(p x) -> p x", p=P),
                             zeros[:, 0:REST]).then_inc(zeroed, 16)
            sp.wait_ge(zeroed, 16 * (FILLS + bool(REST)))

        @block.gpsimd
        def _(pool):
            pool.memset(K.ident[:, :], 0.0).then_inc(masks, 1)
            pool.memset(K.upper[:, :], 1.0).then_inc(masks, 1)
            pool.memset(K.other[:, :], MASKED).then_inc(masks, 1)
            pool.iota(relid_i[:, :], [[0, 1]], base=0, channel_multiplier=1).then_inc(masks, 1)
            pool.wait_ge(masks, 4)
            pool.affine_select(out=K.ident[:, :], in_=K.ident[:, :], compare_op=ALU.not_equal, fill=1.0,
                               base=0, pattern=[[-1, P]], channel_multiplier=1).then_inc(masks, 1)
            pool.affine_select(out=K.upper[:, :], in_=K.upper[:, :], compare_op=ALU.is_ge, fill=0.0,
                               base=0, pattern=[[1, P]], channel_multiplier=-1).then_inc(masks, 1)
            pool.affine_select(out=K.other[:, :].rearrange("r (k q) -> r k q", q=RELS),
                               in_=K.other[:, :].rearrange("r (k q) -> r k q", q=RELS),
                               compare_op=ALU.not_equal, fill=0.0, base=0,
                               pattern=[[0, HEADS], [-1, RELS]], channel_multiplier=1).then_inc(masks, 1)
            pool.wait_ge(ids_in, 16)
            pool.indirect_dma_start(emb[:, :], None, io["rule_emb"],
                                    bass.IndirectOffsetOnAxis(ids[:, 0:1], 0)).then_inc(emb_in, 16)

        @block.vector
        def _(dve):
            dve.memset(zeros[:, :], 0.0).then_inc(cleared, 1)
            dve.memset(K.ones[:, :], 1.0)
            dve.memset(K.quarter[:, :], 1.0 / HEADS)
            dve.memset(K.eps[:, :], EPS)
            dve.memset(heads[:, :], 0.0).then_inc(chain, 1)
            dve.wait_ge(chain, 1)
            for h in range(HEADS):
                q = slice(32 * h, 32 * h + 32)
                ins = dve.memset(heads[q, q], 1.0)
            ins.then_inc(chain, 1)
            dve.wait_ge(chain, 2)
            dve.wait_ge(loaded, 16 * LOADS)
            dve.wait_ge(masks, 7)
            dve.tensor_copy(K.relid[:, :], relid_i[:, :])
            dve.tensor_scalar(K.left[:, :], heads[:, :], al[:, 0:1], None, ALU.mult)
            dve.tensor_scalar(right[:, :], heads[:, :], ar[:, 0:1], None, ALU.mult)
            dve.tensor_reduce(hrel[:, :], K.wr[:, :].rearrange("i (r o) -> i r o", o=P),
                              mybir.AxisListType.X, ALU.add).then_inc(chain, 1)
            dve.wait_ge(chain, 3)
            dve.tensor_scalar(hrelm[:, :], hrel[:, :], 1.0 / P, None, ALU.mult).then_inc(made, 1)
            dve.wait_ge(turned, 3)
            dve.tensor_copy(K.w1t[:, :], pw1[:, 0:P]).then_inc(copied, 1)
            dve.tensor_copy(w2t[:, :], pw2[:, 0:P]).then_inc(copied, 1)
            dve.tensor_copy(embt[:, :], pemb[:, 0:HEADS]).then_inc(copied, 1)
            dve.wait_ge(products, 3)
            dve.tensor_copy(K.w2[:, P:2 * P], pw2r[:, 0:P])
            dve.tensor_copy(vrule[:, :], pv[:, 0:HEADS]).then_inc(chain, 1)
            dve.tensor_tensor(K.krel[:, :], pk[0:RELS, 0:P], wkb[:, :], ALU.add)
            dve.wait_ge(chain, 4)
            dve.tensor_copy(K.rules[:, :].rearrange("f (k r) -> f k r", r=RELS),
                            vrule[:, :].unsqueeze(2).to_broadcast([P, HEADS, RELS]))

        @block.tensor
        def _(pe):
            pe.wait_ge(loaded, 16 * LOADS)
            pe.wait_ge(masks, 7)
            pe.wait_ge(emb_in, 16)
            pe.transpose(pw1[:, 0:P], w1[:, :], K.ident[:, :]).then_inc(turned, 1)
            pe.transpose(pw2[:, 0:P], K.w2[:, 0:P], K.ident[:, :]).then_inc(turned, 1)
            pe.transpose(pemb[:, 0:HEADS], emb[:, :], K.ident[0:HEADS, 0:HEADS]).then_inc(turned, 1)
            pe.wait_ge(copied, 3)
            pe.wait_ge(made, 1)
            pe.matmul(pw2r[:, 0:P], w2t[:, :], right[:, :], start=True, stop=True).then_inc(products, 1)
            pe.matmul(pv[:, 0:HEADS], wk3[:, :], embt[:, :], start=True, stop=True).then_inc(products, 1)
            pe.matmul(pk[0:RELS, 0:P], hrelm[:, :], wk2[:, :], start=True, stop=True).then_inc(products, 1)


def make_indices(K):
    nc, io, sb = K.nc, K.io, K.sb
    NT, NTN, EP = K.NT, K.NTN, K.EP
    K.idx0 = K.dram("idx0", (P, NT), I32)
    K.idx3 = K.dram("idx3", (P, NT), I32)
    K.keep = K.dram("keep", (EP,), BF16)
    K.cap = K.dram("cap", (EP,), BF16)
    K.rel = K.dram("rel", (EP,), BF16)
    K.node_idx = K.dram("node_idx", (NTN, P, 2), I32)
    K.node_inv = K.dram("node_inv", (NTN, P, 2))
    G = 16
    with ExitStack() as t:
        src = sb(t, "src", [P, NT], I32)
        rel8 = sb(t, "rel8", [P, NT], I32)
        rel32 = sb(t, "rel32", [P, NT], I32)
        rows0 = sb(t, "rows0", [P, NT], I32)
        rows3 = sb(t, "rows3", [P, NT], I32)
        cur = sb(t, "cur", [P, NT], I32)
        prev = sb(t, "prev", [P, NT], I32)
        flat32 = sb(t, "flat32", [P, NT], I32)
        keep = sb(t, "keep_s", [P, NT], BF16)
        cap = sb(t, "cap_s", [P, NT], BF16)
        relb = sb(t, "relb", [P, NT], BF16)
        dst = sb(t, "dst", [P, NT], I32)
        hi = sb(t, "hi", [P, NT], I32)
        lo = sb(t, "lo", [P, NT], I32)
        hif = sb(t, "hif", [P, NT])
        lof = sb(t, "lof", [P, NT])
        iota_i = sb(t, "iota_i", [P, P], I32)
        iota_f = sb(t, "iota_f", [P, P])
        node_i = sb(t, "node_i", [P, NTN], I32)
        node_f = sb(t, "node_f", [P, NTN])
        ohlo = sb(t, "ohlo", [P, 2, G, P], BF16)
        ohhi = sb(t, "ohhi", [P, 2, G, NTN], BF16)
        cnt = sb(t, "cnt", [P, NTN])
        tot = sb(t, "tot", [P, NTN])
        run_tot = sb(t, "run_tot", [P, NTN])
        onesn = sb(t, "onesn", [P, NTN])
        w = [sb(t, f"nw{n}", [P, NTN]) for n in range(8)]
        nidx = sb(t, "nidx", [P, NTN, 2], I32)
        ninv = sb(t, "ninv", [P, NTN, 2])
        pc = [K.bank(t, f"pc{n}", (P, 512)) for n in range(2)]
        pin, ptot = K.bank(t, "pin"), K.bank(t, "ptot")
        loaded, stored, made, iotas = K.sem(t, "i_loaded"), K.sem(t, "i_stored"), K.sem(t, "i_made"), K.sem(t, "i_iotas")
        onehot, counted, added = K.sem(t, "i_onehot"), K.sem(t, "i_counted"), K.sem(t, "i_added")
        prefix, chain = K.sem(t, "i_prefix"), K.sem(t, "i_chain")
        STEPS = NT // G
        block = K.phase(t)

        @block.sync
        def _(sp):
            for a, b in ((src, io["src_t"]), (rel8, io["rel8_t"]), (rel32, io["rel32_t"]), (dst, io["dst_t"]),
                         (cur, io["dst"][1:EP + 1].rearrange("(p j) -> p j", p=P)),
                         (prev, io["dst"][0:EP].rearrange("(p j) -> p j", p=P)),
                         (flat32, io["rel32"].rearrange("(p j) -> p j", p=P))):
                sp.dma_start(a[:, :], b).then_inc(loaded, 16)
            sp.wait_ge(made, 1)
            sp.dma_start(K.idx0, rows0[:, :]).then_inc(stored, 16)
            sp.dma_start(K.idx3, rows3[:, :]).then_inc(stored, 16)
            for a, b in ((keep, K.keep), (cap, K.cap), (relb, K.rel)):
                sp.dma_start(b.rearrange("(p j) -> p j", p=P), a[:, :]).then_inc(stored, 16)
            sp.wait_ge(made, 2)
            sp.dma_start(K.node_idx.rearrange("t p a -> p t a"), nidx[:, :, :]).then_inc(stored, 16)
            sp.dma_start(K.node_inv.rearrange("t p a -> p t a"), ninv[:, :, :]).then_inc(stored, 16)
            sp.wait_ge(stored, 16 * 7)

        @block.gpsimd
        def _(pool):
            pool.iota(iota_i[:, :], [[1, P]], base=0, channel_multiplier=0).then_inc(iotas, 1)
            pool.iota(node_i[:, :], [[P, NTN]], base=EP, channel_multiplier=1).then_inc(iotas, 1)

        @block.vector
        def _(dve):
            n = [0]

            def link(ins):
                n[0] += 1
                ins.then_inc(chain, 1)
                dve.wait_ge(chain, n[0])

            dve.wait_ge(loaded, 16 * 7)
            dve.wait_ge(iotas, 2)
            dve.scalar_tensor_tensor(rows0[:, :], src[:, :], float(RELS0), rel8[:, :], ALU.mult, ALU.add)
            dve.scalar_tensor_tensor(rows3[:, :], src[:, :], float(RELS), rel32[:, :], ALU.mult, ALU.add)
            dve.tensor_copy(relb[:, :], flat32[:, :])
            link(dve.tensor_tensor(keep[:, :], cur[:, :], prev[:, :], ALU.is_equal))
            dve.tensor_scalar(cap[:, :], keep[:, :], 2 * HUGE / 2, -HUGE / 2, ALU.mult, ALU.add).then_inc(made, 1)
            dve.tensor_scalar(hi[:, :], dst[:, :], 7, None, ALU.logical_shift_right)
            link(dve.tensor_scalar(lo[:, :], dst[:, :], P - 1, None, ALU.bitwise_and))
            dve.tensor_copy(hif[:, :], hi[:, :])
            dve.tensor_copy(lof[:, :], lo[:, :])
            dve.tensor_copy(iota_f[:, :], iota_i[:, :])
            dve.tensor_copy(node_f[:, :], node_i[:, :])
            dve.memset(onesn[:, :], 1.0)
            link(dve.memset(cnt[:, :], 0.0))

            def hot(s):
                dve.wait_ge(counted, done(s, 2))
                at = bass.ds(s.n * G, G)
                dve.tensor_tensor(ohlo[:, s.k, :, :], iota_f[:, :].unsqueeze(1).to_broadcast([P, G, P]),
                                  lof[:, at].unsqueeze(2).to_broadcast([P, G, P]), ALU.is_equal)
                dve.tensor_tensor(ohhi[:, s.k, :, :], iota_f[:, 0:NTN].unsqueeze(1).to_broadcast([P, G, NTN]),
                                  hif[:, at].unsqueeze(2).to_broadcast([P, G, NTN]),
                                  ALU.is_equal).then_inc(onehot, 1)

            def add(s):
                dve.wait_ge(counted, done(s))
                dve.wait_ge(added, done(s, 1))
                dve.tensor_tensor(cnt[:, :], cnt[:, :], pc[s.k][:, 0:NTN], ALU.add).then_inc(added, 1)

            dve.sem_inc(onehot, CREDIT)
            dve.sem_inc(added, CREDIT)
            run(dve, STEPS, 2, [(hot, 0), (add, -1)])
            dve.wait_ge(added, STEPS + CREDIT)
            dve.wait_ge(prefix, 2)
            dve.tensor_copy(w[0][:, :], pin[:, 0:NTN])
            link(dve.tensor_copy(tot[:, :], ptot[:, 0:NTN]))
            link(dve.tensor_tensor_scan(run_tot[:, :], onesn[:, :], tot[:, :], 0.0, ALU.mult, ALU.add))
            link(dve.tensor_tensor(w[1][:, :], run_tot[:, :], tot[:, :], ALU.subtract))
            link(dve.tensor_tensor(w[2][:, :], w[0][:, :], w[1][:, :], ALU.add))
            dve.tensor_scalar(nidx[:, :, 0], w[2][:, :], -1.0, 0.0, ALU.add, ALU.max)
            link(dve.tensor_tensor(w[3][:, :], w[2][:, :], cnt[:, :], ALU.subtract))
            link(dve.tensor_scalar(w[4][:, :], cnt[:, :], 1.0, None, ALU.min))
            dve.tensor_copy(ninv[:, :, 0], w[4][:, :])
            link(dve.tensor_tensor(w[5][:, :], w[3][:, :], node_f[:, :], ALU.subtract))
            link(dve.tensor_tensor(w[6][:, :], w[5][:, :], w[4][:, :], ALU.mult))
            dve.tensor_tensor(nidx[:, :, 1], w[6][:, :], node_f[:, :], ALU.add)
            link(dve.tensor_scalar(w[7][:, :], cnt[:, :], 1.0, None, ALU.max))
            link(dve.reciprocal(w[0][:, :], w[7][:, :]))
            dve.tensor_tensor(ninv[:, :, 1], w[0][:, :], w[4][:, :], ALU.mult).then_inc(chain, 1)
            n[0] += 1
            dve.wait_ge(chain, n[0])
            dve.tensor_copy(w[1][:, 0:1], w[0][:, 0:1]).then_inc(made, 1)

        @block.tensor
        def _(pe):
            def count(s):
                pe.wait_ge(onehot, done(s))
                pe.wait_ge(added, done(s, 2))
                for g in range(G):
                    ins = pe.matmul(pc[s.k][:, 0:NTN], ohlo[:, s.k, g, :], ohhi[:, s.k, g, :],
                                    start=(g == 0), stop=(g == G - 1))
                ins.then_inc(counted, 1)

            pe.sem_inc(counted, CREDIT)
            run(pe, STEPS, 2, [(count, 0)])
            pe.wait_ge(added, STEPS + CREDIT)
            pe.matmul(pin[:, 0:NTN], K.upper[:, :], cnt[:, :], start=True, stop=True).then_inc(prefix, 1)
            pe.matmul(ptot[:, 0:NTN], K.ones[:, :], cnt[:, :], start=True, stop=True).then_inc(prefix, 1)


def hold(eng, carrier, sem, value):
    eng.wait_ge(sem, value)
    eng.sem_inc(carrier, 1)


def edge_pass(K, name, kind, table, idx, rows_out, scores=None):
    nc, sb, NB = K.nc, K.sb, K.NB
    fills = kind in ("gat", "rel", "mix")
    soft = kind in ("gat", "rel")
    W = 2 if soft else 1
    with ExitStack() as t:
        S = lambda what: K.sem(t, f"{name}_{what}")

        def ring(what, shape=(P, B), dt=F32):
            return [sb(t, f"{name}_{what}{k}", list(shape), dt) for k in range(RING)]

        ix = ring("ix", (P, T), I32)
        g = ring("g", (P, T, P))
        o = ring("o")
        out = ring("out", (P, T, W * P))
        first = ring("first", (P, T, P)) if fills else None
        spread = ring("spread") if fills else None
        keep = ring("keepr", dt=BF16) if kind != "max" else None
        cap = ring("capr", dt=BF16) if kind == "max" or soft else None
        if soft:
            sc = sb(t, f"{name}_sc", [P, 1 + RING * B])
            mprev, d, grow, a, ss = (ring(x) for x in ("mprev", "d", "grow", "a", "ss"))
        if kind == "gat":
            gs, t2 = ring("gs"), ring("t2")
        if kind == "rel":
            relr = ring("relr", (RELS, B), BF16)
            hot = ring("hot", (RELS, B))
            prod = ring("prod")
        if kind == "mix":
            scr, d, a, at, am = (ring(x) for x in ("scr", "d", "a", "at", "am"))
        NG = 4 if kind == "mix" else 2
        pg = [K.bank(t, f"{name}_pg{n}") for n in range(NG)]
        pf = [K.bank(t, f"{name}_pf{n}") for n in range(2)] if fills else None
        ps = [K.bank(t, f"{name}_ps{n}") for n in range(1 if kind == "mix" else 2)] if fills else None
        NS = len(ps) if fills else 0
        po = [K.bank(t, f"{name}_po{n}") for n in range(W)]

        s_ix = [S(f"ix{k}") for k in range(RING)]
        s_in = [S(f"in{k}") for k in range(RING)]
        s_g = [S(f"g{k}") for k in range(RING)]
        s_out = [S(f"out{k}") for k in range(RING)]
        s_sc = [S(f"sc{k}") for k in range(RING)] if kind == "rel" else None
        turned = S("turned")
        turned_first = S("turned_first")
        scored = S("scored")
        back = S("back")
        filled = S("filled")
        hotted = S("hotted")
        prodded = S("prodded")
        sced = S("sced")
        maxed = S("maxed")
        diffed = S("diffed")
        negd = S("negd")
        weighed = S("weighed")
        summed = S("summed")
        scanned = S("scanned")
        copied = S("copied")
        scaled = S("scaled")
        relued = S("relued")
        grown = S("grown")
        exped = S("exped")
        evac = S("evac")
        n_in = (1 if kind == "max" else 1 + soft) + fills + (kind in ("rel", "mix"))
        last = S("last")
        issued = S("issued")
        free = S("free")

        block = K.phase(t)
        at_edges = lambda ap, s: ap[bass.ds(s.n * B, B)]

        @block.sync
        def _(sp):
            def load_ix(s):
                hold(sp, free, s_g[s.k], 16 * T * s.turn)
                sp.dma_start(ix[s.k][:, :], idx[:, bass.ds(s.n * T, T)]).then_inc(s_ix[s.k], 16)

            def load_in(s):
                hold(sp, free, maxed if soft else scanned, done(s, RING))
                if fills:
                    hold(sp, free, turned_first, done(s, RING))
                    hold(sp, free, filled, done(s, RING))
                if kind == "rel":
                    hold(sp, free, hotted, done(s, RING))
                if kind == "mix":
                    hold(sp, free, diffed, done(s, RING))
                if keep:
                    sp.dma_start(keep[s.k][:, :], at_edges(K.keep, s).partition_broadcast(P)).then_inc(s_in[s.k], 16)
                if cap:
                    sp.dma_start(cap[s.k][:, :], at_edges(K.cap, s).partition_broadcast(P)).then_inc(s_in[s.k], 16)
                if fills:
                    sp.dma_start(first[s.k][:, :, :], K.first_rows[bass.ds(s.n * B, B), :]
                                 .rearrange("(t p) f -> p t f", p=P)).then_inc(s_in[s.k], 16)
                if kind == "rel":
                    sp.dma_start(relr[s.k][:, :], at_edges(K.rel, s).partition_broadcast(RELS)).then_inc(s_in[s.k], 16)
                if kind == "mix":
                    sp.dma_start(scr[s.k][:, :], scores[bass.ds(s.n * P, P), :]).then_inc(s_in[s.k], 16)

            run(sp, NB, RING, [(load_ix, 1), (load_in, 0)])

        @block.gpsimd
        def _(pool):
            def gather(s):
                pool.wait_ge(s_ix[s.k], 16 * (s.turn + 1))
                pool.wait_ge(turned, done(s, RING))
                pool.sem_inc(issued, 1)
                for j in range(T):
                    pool.indirect_dma_start(g[s.k][:, j, :], None, table,
                                            bass.IndirectOffsetOnAxis(ix[s.k][:, j:j + 1], 0)).then_inc(s_g[s.k], 16)

            run(pool, NB, RING, [(gather, 0)])

        @block.tensor
        def _(pe):
            def turn(s):
                pe.wait_ge(s_g[s.k], 16 * T * (s.turn + 1))
                if kind in ("max", "sum"):
                    pe.wait_ge(scanned, done(s, NG))
                elif kind == "gat":
                    pe.wait_ge(copied, done(s, NG))
                elif kind == "rel":
                    pe.wait_ge(prodded, done(s, NG))
                else:
                    pe.wait_ge(weighed, done(s, NG))
                bank = pg[s.k % NG]
                if kind == "rel":
                    pe.wait_ge(hotted, done(s))
                    pe.matmul(bank[:, :], K.krel[:, :], hot[s.k][:, :], start=True, stop=False)
                    for j in range(T):
                        ins = pe.matmul(bank[:, j * P:(j + 1) * P], g[s.k][:, j, :], K.ident[:, :],
                                        start=False, stop=(j == T - 1))
                else:
                    for j in range(T):
                        ins = pe.transpose(bank[:, j * P:(j + 1) * P], g[s.k][:, j, :], K.ident[:, :])
                ins.then_inc(turned, 1)

            def turn_first(s):
                pe.wait_ge(s_in[s.k], 16 * n_in * (s.turn + 1))
                pe.wait_ge(filled, done(s, 2))
                for j in range(T):
                    ins = pe.transpose(pf[s.k % 2][:, j * P:(j + 1) * P], first[s.k][:, j, :], K.ident[:, :])
                ins.then_inc(turned_first, 1)

            def score(s):
                bank = ps[s.k % NS]
                if kind == "gat":
                    pe.wait_ge(sced, done(s, NS))
                    pe.wait_ge(scaled, done(s, NS))
                    pe.wait_ge(copied, done(s))
                    pe.wait_ge(filled, done(s))
                    pe.matmul(bank[:, :], K.left[:, :], gs[s.k][:, :], start=True, stop=False)
                    pe.matmul(bank[:, :], K.ident[:, :], spread[s.k][:, :], start=False, stop=True).then_inc(scored, 1)
                elif kind == "rel":
                    pe.wait_ge(sced, done(s, NS))
                    pe.wait_ge(prodded, done(s))
                    pe.matmul(bank[:, :], K.ones[:, :], prod[s.k][:, :], start=True, stop=False)
                    pe.matmul(bank[:, :], K.rules[:, :], spread[s.k][:, :], start=False, stop=False)
                    pe.matmul(bank[:, :], K.other[:, :], hot[s.k][:, :], start=False, stop=True).then_inc(scored, 1)
                else:
                    pe.wait_ge(copied, done(s, NS))
                    pe.wait_ge(exped, done(s))
                    pe.matmul(bank[:, :], K.quarter[:, :], a[s.k][:, :], start=True, stop=True).then_inc(scored, 1)

            def turn_back(s):
                pe.wait_ge(evac, done(s, 1))
                pe.wait_ge(weighed if kind == "rel" else scanned, done(s))
                for j in range(T):
                    ins = pe.transpose(po[0][:, j * P:(j + 1) * P], o[s.k][:, j * P:(j + 1) * P], K.ident[:, :])
                if soft:
                    pe.wait_ge(summed, done(s))
                    for j in range(T):
                        ins = pe.transpose(po[1][:, j * P:(j + 1) * P], ss[s.k][:, j * P:(j + 1) * P], K.ident[:, :])
                ins.then_inc(back, 1)

            for x in (turned, turned_first, scored, back):
                pe.sem_inc(x, CREDIT)
            if soft:
                run(pe, NB, RING, [(turn, 2), (turn_first, 2), (score, 1), (turn_back, -2)])
            elif fills:
                run(pe, NB, RING, [(turn, 2), (turn_first, 2), (score, 1), (turn_back, -1)])
            else:
                run(pe, NB, RING, [(turn, 1), (turn_back, -1)])

        @block.vector
        def _(dve):
            def one_hot(s):
                dve.wait_ge(s_in[s.k], 16 * n_in * (s.turn + 1))
                dve.wait_ge(scored, done(s, RING))
                dve.tensor_scalar(hot[s.k][:, :], relr[s.k][:, :], K.relid[:, 0:1], None,
                                  ALU.is_equal).then_inc(hotted, 1)

            def fill(s):
                dve.wait_ge(s_in[s.k], 16 * n_in * (s.turn + 1))
                dve.wait_ge(turned_first, done(s))
                dve.wait_ge(filled, done(s, 1))
                if kind != "mix":
                    dve.wait_ge(scored, done(s, RING))
                dve.tensor_tensor_scan(spread[s.k][:, :], keep[s.k][:, :], pf[s.k % 2][:, :],
                                       spread[s.prev][:, B - 1:B], ALU.mult, ALU.add).then_inc(filled, 1)

            def key_query(s):
                dve.wait_ge(turned, done(s))
                dve.wait_ge(filled, done(s))
                dve.wait_ge(scored, done(s, RING))
                dve.tensor_tensor(prod[s.k][:, :], pg[s.k % 2][:, :], spread[s.k][:, :], ALU.mult).then_inc(prodded, 1)

            def running_max(s):
                here = slice(1 + B * s.k, 1 + B * (s.k + 1))
                if kind == "gat":
                    dve.wait_ge(scaled, done(s))
                    dve.wait_ge(diffed, done(s, RING))
                    dve.tensor_tensor(sc[:, here], ps[s.k % NS][:, :], t2[s.k][:, :], ALU.max).then_inc(sced, 1)
                dve.wait_ge(sced, done(s))
                dve.wait_ge(maxed, done(s, 1))
                if s.k == 0:
                    dve.wait_ge(last, s.turn + 1)
                dve.tensor_tensor_scan(mprev[s.k][:, :], sc[:, B * s.k:B * (s.k + 1)], cap[s.k][:, :],
                                       mprev[s.prev][:, B - 1:B], ALU.max, ALU.min).then_inc(maxed, 1)
                dve.wait_ge(maxed, done(s))
                if s.k == RING - 1:
                    dve.tensor_copy(sc[:, 0:1], sc[:, RING * B:RING * B + 1]).then_inc(last, 1)
                dve.wait_ge(relued, done(s, RING))
                dve.tensor_tensor(d[s.k][:, :], sc[:, here], mprev[s.k][:, :], ALU.subtract).then_inc(diffed, 1)
                dve.wait_ge(diffed, done(s))
                dve.tensor_scalar(a[s.k][:, :], d[s.k][:, :], 0.0, None, ALU.min).then_inc(negd, 1)
                if kind == "rel":
                    dve.wait_ge(back, done(s, RING))
                    dve.tensor_tensor(o[s.k][:, :], sc[:, here], mprev[s.k][:, :], ALU.max).then_inc(weighed, 1)

            def soft_sums(s):
                dve.wait_ge(exped, done(s))
                dve.wait_ge(grown, done(s))
                if kind == "gat":
                    dve.tensor_tensor(gs[s.k][:, :], a[s.k][:, :], gs[s.k][:, :], ALU.mult).then_inc(weighed, 1)
                dve.wait_ge(back, done(s, RING))
                dve.wait_ge(summed, done(s, 1))
                dve.tensor_tensor_scan(ss[s.k][:, :], grow[s.k][:, :], a[s.k][:, :],
                                       ss[s.prev][:, B - 1:B], ALU.mult, ALU.add).then_inc(summed, 1)
                if kind == "gat":
                    dve.wait_ge(weighed, done(s))
                    dve.wait_ge(scanned, done(s, 1))
                    dve.tensor_tensor_scan(o[s.k][:, :], grow[s.k][:, :], gs[s.k][:, :],
                                           o[s.prev][:, B - 1:B], ALU.mult, ALU.add).then_inc(scanned, 1)

            def scan_rows(s):
                dve.wait_ge(s_in[s.k], 16 * n_in * (s.turn + 1))
                dve.wait_ge(turned, done(s))
                dve.wait_ge(back, done(s, RING))
                dve.wait_ge(scanned, done(s, 1))
                mark, op0, op1 = (cap, ALU.min, ALU.max) if kind == "max" else (keep, ALU.mult, ALU.add)
                dve.tensor_tensor_scan(o[s.k][:, :], mark[s.k][:, :], pg[s.k % NG][:, :],
                                       o[s.prev][:, B - 1:B], op0, op1).then_inc(scanned, 1)

            def attention(s):
                dve.wait_ge(filled, done(s))
                dve.wait_ge(exped, done(s, RING))
                dve.tensor_tensor(d[s.k][:, :], scr[s.k][:, :], spread[s.k][:, :], ALU.subtract).then_inc(diffed, 1)

            def mix_rows(s):
                dve.wait_ge(copied, done(s))
                dve.wait_ge(turned, done(s))
                dve.tensor_tensor(am[s.k][:, :], pg[s.k % NG][:, :], at[s.k][:, :], ALU.mult).then_inc(weighed, 1)
                dve.wait_ge(weighed, done(s))
                dve.wait_ge(back, done(s, RING))
                dve.wait_ge(scanned, done(s, 1))
                dve.tensor_tensor_scan(o[s.k][:, :], keep[s.k][:, :], am[s.k][:, :],
                                       o[s.prev][:, B - 1:B], ALU.mult, ALU.add).then_inc(scanned, 1)

            for x, v in ((o, -HUGE if kind == "max" else 0.0), (spread, 0.0),
                         *(((mprev, -HUGE), (ss, 0.0)) if soft else ())):
                if x:
                    dve.memset(x[RING - 1][:, B - 1:B], v)
            if soft:
                dve.memset(sc[:, 0:1], 0.0)
            dve.memset(o[0][:, 0:1], 0.0).then_inc(last, 1)
            dve.wait_ge(last, 1)
            mine = [filled, hotted, prodded, maxed, diffed, negd, weighed, summed, scanned]
            for x in mine + ([sced] if kind == "gat" else []):
                dve.sem_inc(x, CREDIT)
            if kind == "gat":
                run(dve, NB, RING, [(fill, 1), (running_max, 0), (soft_sums, -1)])
            elif kind == "rel":
                run(dve, NB, RING, [(one_hot, 2), (fill, 1), (key_query, 1), (running_max, 0), (soft_sums, -1)])
            elif kind == "mix":
                run(dve, NB, RING, [(fill, 2), (attention, 2), (mix_rows, 0)])
            else:
                run(dve, NB, RING, [(scan_rows, 0)])

        @block.scalar
        def _(act):
            def copy_rows(s):
                act.wait_ge(turned, done(s))
                act.wait_ge(scored, done(s, RING))
                act.wait_ge(scanned, done(s, RING))
                act.activation(gs[s.k][:, :], pg[s.k % NG][:, :], ACT.Copy).then_inc(copied, 1)

            def scores_in(s):
                act.wait_ge(scored, done(s))
                if kind == "gat":
                    act.wait_ge(sced, done(s, RING))
                    act.activation(t2[s.k][:, :], ps[s.k % NS][:, :], ACT.Copy, scale=SLOPE).then_inc(scaled, 1)
                else:
                    act.wait_ge(diffed, done(s, RING))
                    act.wait_ge(maxed, done(s, RING - 1))
                    act.wait_ge(weighed, done(s, RING))
                    if s.k == RING - 1:
                        act.wait_ge(last, s.turn + 1)
                    act.wait_ge(s_sc[s.k], 16 * s.turn)
                    act.activation(sc[:, 1 + B * s.k:1 + B * (s.k + 1)], ps[s.k % NS][:, :], ACT.Copy,
                                   scale=float(P) ** -0.5).then_inc(sced, 1)
                    act.wait_ge(sced, done(s))
                    act.dma_start(scores[bass.ds(s.n * P, P), :],
                                  sc[:, 1 + B * s.k:1 + B * (s.k + 1)]).then_inc(s_sc[s.k], 16)

            def exps(s):
                act.wait_ge(diffed, done(s))
                act.wait_ge(scanned if kind == "gat" else summed, done(s, RING))
                act.activation(grow[s.k][:, :], d[s.k][:, :], ACT.Relu).then_inc(relued, 1)
                act.wait_ge(negd, done(s))
                act.activation(a[s.k][:, :], a[s.k][:, :], ACT.Exp).then_inc(exped, 1)
                act.wait_ge(relued, done(s))
                act.activation(grow[s.k][:, :], grow[s.k][:, :], ACT.Exp, scale=-1.0).then_inc(grown, 1)

            def exp_mix(s):
                act.wait_ge(diffed, done(s))
                act.wait_ge(scored, done(s, RING))
                act.activation(a[s.k][:, :], d[s.k][:, :], ACT.Exp).then_inc(exped, 1)

            def copy_mix(s):
                act.wait_ge(scored, done(s))
                act.wait_ge(weighed, done(s, RING))
                act.activation(at[s.k][:, :], ps[s.k % NS][:, :], ACT.Copy).then_inc(copied, 1)

            def store(s):
                act.wait_ge(back, done(s))
                act.wait_ge(s_out[s.k], 16 * s.turn)
                for w in range(W):
                    ins = act.activation(out[s.k][:, :, w * P:(w + 1) * P],
                                         po[w][:, :].rearrange("p (t f) -> p t f", f=P), ACT.Copy)
                ins.then_inc(evac, 1)
                act.wait_ge(evac, done(s))
                act.dma_start(rows_out[bass.ds(s.n * B, B), 0:W * P].rearrange("(t p) f -> p t f", p=P),
                              out[s.k][:, :, :]).then_inc(s_out[s.k], 16)

            for x in [copied, scaled, relued, grown, exped, evac] + ([] if kind == "gat" else [sced]):
                act.sem_inc(x, CREDIT)
            if kind == "gat":
                run(act, NB, RING, [(copy_rows, 2), (scores_in, 1), (exps, 0), (store, -2)])
            elif kind == "rel":
                run(act, NB, RING, [(scores_in, 1), (exps, 0), (store, -2)])
            elif kind == "mix":
                run(act, NB, RING, [(exp_mix, 2), (copy_mix, 1), (store, -1)])
            else:
                run(act, NB, RING, [(store, -1)])
            for k in range(RING):
                act.wait_ge(s_out[k], 16 * (NB // RING))
                if kind == "rel":
                    act.wait_ge(s_sc[k], 16 * (NB // RING))


def node_phase(K, name, kind, rows_in, x_in=None, x_out=None, self_in=None, self_out=None, table=None,
               table3=None):
    nc, sb, NTN = K.nc, K.sb, K.NTN
    R = 2
    W = 2 if kind in ("gat", "lse") else 1
    scatters = kind in ("sum", "gat", "lse")
    gathers = kind != "start"
    normed = kind not in ("start", "lse")
    makes = kind in ("start", "max", "sum", "gat")
    cols = {"start": (RELS0 + 1) * P, "max": P, "sum": 2 * P, "gat": 2 * P}.get(kind, P)
    wide = RELS * P // B
    with ExitStack() as t:
        S = lambda what: K.sem(t, f"{name}_{what}")

        def ring(what, shape=(P, P), dt=F32):
            return [sb(t, f"{name}_{what}{k}", list(shape), dt) for k in range(R)]

        ids, inv = ring("ids", (P, 2), I32), ring("inv", (P, 2))
        x, own, rows = ring("x"), ring("own"), ring("rows", (P, W * P))
        u, v, w_, y, z = (ring(n) for n in ("u", "v", "w", "y", "z"))
        stats, mv, sd, rsd = ring("stats", (P, 6)), ring("mv", (P, 2)), ring("sd", (P, 1)), ring("rsd", (P, 1))
        xn = ring("xn")
        xt = ring("xt")
        h = ring("h", (P, cols))
        big = ring("big", (P, RELS * P)) if kind == "gat" else None
        pt = [K.bank(t, f"{name}_pt{k}") for k in range(2)]
        NPM = 3 if kind == "start" else 1
        pm = [K.bank(t, f"{name}_pm{k}") for k in range(NPM)]
        pw = [K.bank(t, f"{name}_pw{k}") for k in range(4)] if kind == "gat" else None
        s_ld = [S(f"ld{k}") for k in range(R)]
        s_rows = [S(f"rows{k}") for k in range(R)]
        s_sc = [S(f"sc{k}") for k in range(R)]
        s_st = [S(f"st{k}") for k in range(R)]
        n_ld = 2 * gathers + (kind != "lse") + (kind == "max")
        n_st = {"start": 2, "max": 2, "sum": 2, "gat": 3, "lse": 0, "mix": 1}[kind]
        chain = S("chain")
        fresh = S("fresh")
        spread_v = S("spread_v")
        spread_d = S("spread_d")
        logged = S("logged")
        turned, flipped = S("turned"), S("flipped")
        product, made = S("product"), S("made")
        wprod, wmade = S("wprod"), S("wmade")
        wmade_a = S("wmade_a")
        issued = S("issued")
        carried = S("carried")
        free = S("free")
        block = K.phase(t)
        rows_of = lambda ap, s: ap[bass.ds(s.n * P, P), :]
        NORMS = {"max": 1, "sum": 1, "gat": 1, "mix": 2}.get(kind, 0)
        result = x if kind == "start" else xn

        @block.sync
        def _(sp):
            def load(s):
                hold(sp, free, fresh, done(s, R))
                if makes:
                    hold(sp, free, turned, done(s, R))
                if gathers:
                    hold(sp, free, s_rows[s.k], 16 * s.turn)
                    if scatters:
                        hold(sp, free, s_sc[s.k], 16 * s.turn)
                if gathers:
                    sp.dma_start(ids[s.k][:, :], K.node_idx[bass.ds(s.n, 1), :, :]
                                 .rearrange("o p a -> (o p) a")).then_inc(s_ld[s.k], 16)
                    sp.dma_start(inv[s.k][:, :], K.node_inv[bass.ds(s.n, 1), :, :]
                                 .rearrange("o p a -> (o p) a")).then_inc(s_ld[s.k], 16)
                if kind != "lse":
                    sp.dma_start(x[s.k][:, :], rows_of(x_in, s)).then_inc(s_ld[s.k], 16)
                if kind == "max":
                    sp.dma_start(own[s.k][:, :], rows_of(self_in, s)).then_inc(s_ld[s.k], 16)

            def store(s):
                if n_st == 0:
                    return
                if kind != "start":
                    hold(sp, free, fresh, done(s))
                    sp.dma_start(rows_of(x_out, s), xn[s.k][:, :]).then_inc(s_st[s.k], 16)
                if makes:
                    hold(sp, free, made, done(s))
                if kind == "start":
                    sp.dma_start(table[bass.ds(s.n * P * RELS0, P * RELS0), :].rearrange("(p r) f -> p r f", p=P),
                                 h[s.k][:, 0:RELS0 * P].rearrange("p (r f) -> p r f", f=P)).then_inc(s_st[s.k], 16)
                    sp.dma_start(rows_of(self_out, s), h[s.k][:, RELS0 * P:]).then_inc(s_st[s.k], 16)
                elif makes:
                    sp.dma_start(rows_of(table, s), h[s.k][:, 0:P]).then_inc(s_st[s.k], 16)
                if kind == "gat":
                    hold(sp, free, wmade, s.n * (wide // 2) + wide // 2)
                    hold(sp, free, wmade_a, s.n * (wide // 2) + wide // 2)
                    sp.dma_start(table3[bass.ds(s.n * P * RELS, P * RELS), :].rearrange("(p r) f -> p r f", p=P),
                                 big[s.k][:, :].rearrange("p (r f) -> p r f", f=P)).then_inc(s_st[s.k], 16)

            run(sp, NTN, R, [(load, 1), (store, -1)])
            for k in range(R):
                sp.wait_ge(s_st[k], 16 * n_st * (NTN // R))

        @block.gpsimd
        def _(pool):
            def gather(s):
                pool.wait_ge(s_ld[s.k], 16 * n_ld * (s.turn + 1))
                pool.wait_ge(fresh, done(s, R))
                pool.sem_inc(issued, 1)
                pool.indirect_dma_start(rows[s.k][:, :], None, rows_in[:, 0:W * P],
                                        bass.IndirectOffsetOnAxis(ids[s.k][:, 0:1], 0)).then_inc(s_rows[s.k], 16)

            def scatter(s):
                if kind == "lse":
                    pool.wait_ge(fresh, done(s))
                    rows_ = xn[s.k][:, :]
                else:
                    pool.wait_ge(made, done(s))
                    rows_ = h[s.k][:, P:2 * P]
                pool.sem_inc(issued, 1)
                pool.indirect_dma_start(K.first_rows, bass.IndirectOffsetOnAxis(ids[s.k][:, 1:2], 0),
                                        rows_, None).then_inc(s_sc[s.k], 16)

            if scatters:
                run(pool, NTN, R, [(scatter, -1), (gather, 1)])
                for k in range(R):
                    pool.wait_ge(s_sc[k], 16 * (NTN // R))
            elif gathers:
                run(pool, NTN, R, [(gather, 0)])

        @block.tensor
        def _(pe):
            def turn(s):
                if kind == "start":
                    pe.wait_ge(s_ld[s.k], 16 * n_ld * (s.turn + 1))
                else:
                    pe.wait_ge(fresh, done(s))
                pe.wait_ge(flipped, done(s, 2))
                pe.transpose(pt[s.k][:, 0:P], result[s.k][:, :], K.ident[:, :]).then_inc(turned, 1)

            def multiply(s):
                pe.wait_ge(flipped, done(s))
                pe.wait_ge(made, done(s, 1))
                w = {"start": K.w0, "max": K.w1t, "sum": K.w2, "gat": K.wkq}[kind]
                for c in range(0, cols, B):
                    n = min(B, cols - c)
                    ins = pe.matmul(pm[c // B][:, 0:n], xt[s.k][:, :], w[:, c:c + n], start=True, stop=True)
                ins.then_inc(product, 1)
                if kind == "gat":
                    for c in range(wide):
                        sem, n = (wmade, wmade_a)[c % 2], c // 2
                        if n or not isinstance(s.n, int) or s.n:
                            pe.wait_ge(sem, s.n * (wide // 2) + (n - 1))
                        pe.matmul(pw[c % 4][:, :], xt[s.k][:, :], K.wr[:, c * B:(c + 1) * B],
                                  start=True, stop=True).then_inc(wprod, 1)

            if makes:
                for q in (turned, product):
                    pe.sem_inc(q, CREDIT)
                run(pe, NTN, R, [(multiply, -1), (turn, 0)])

        @block.vector
        def _(dve):
            per = {"max": 2, "sum": 2, "gat": 4, "lse": 3, "mix": 4}.get(kind, 0) + 4 * NORMS
            c = [0]

            def link(s, ins):
                c[0] += 1
                ins.then_inc(chain, 1)
                dve.wait_ge(chain, s.n * per + c[0])

            norm_no = [0]

            def norm(s, out, in_):
                norm_no[0] += 1
                link(s, dve.bn_stats(stats[s.k][:, :], in_))
                dve.sem_inc(carried, 1)
                link(s, dve.bn_aggr(mv[s.k][:, :], stats[s.k][:, :]))
                dve.tensor_scalar(rsd[s.k][:, :], mv[s.k][:, 1:2], EPS, None, ALU.add).then_inc(spread_v, 1)
                dve.wait_ge(spread_d, s.n * NORMS + norm_no[0])
                link(s, dve.reciprocal(rsd[s.k][:, :], sd[s.k][:, :]))
                return dve.tensor_scalar(out, in_, mv[s.k][:, 0:1], rsd[s.k][:, 0:1], ALU.subtract, ALU.mult)

            def finish(s):
                c[0] = norm_no[0] = 0
                dve.wait_ge(s_rows[s.k], 16 * (s.turn + 1))
                dve.wait_ge(s_ld[s.k], 16 * n_ld * (s.turn + 1))
                if makes:
                    dve.wait_ge(turned, done(s, R))
                if n_st:
                    dve.wait_ge(s_st[s.k], 16 * n_st * s.turn)
                if kind == "lse":
                    dve.wait_ge(s_sc[s.k], 16 * s.turn)
                k = s.k
                if kind == "max":
                    link(s, dve.scalar_tensor_tensor(u[k][:, :], rows[k][:, :], inv[k][:, 0:1], own[k][:, :],
                                                     ALU.mult, ALU.add))
                    link(s, dve.scalar_tensor_tensor(y[k][:, :], u[k][:, :], 0.0, x[k][:, :], ALU.max, ALU.add))
                elif kind == "sum":
                    link(s, dve.tensor_scalar(u[k][:, :], rows[k][:, :], inv[k][:, 1:2], 0.0, ALU.mult, ALU.max))
                    link(s, dve.tensor_tensor(y[k][:, :], u[k][:, :], x[k][:, :], ALU.add))
                elif kind == "gat":
                    link(s, dve.reciprocal(u[k][:, :], rows[k][:, P:2 * P]))
                    link(s, dve.tensor_tensor(v[k][:, :], rows[k][:, 0:P], u[k][:, :], ALU.mult))
                    link(s, dve.scalar_tensor_tensor(w_[k][:, :], v[k][:, :], inv[k][:, 0:1], K.b2[:, :],
                                                     ALU.mult, ALU.add))
                    link(s, dve.tensor_tensor(y[k][:, :], w_[k][:, :], x[k][:, :], ALU.add))
                elif kind == "lse":
                    link(s, dve.tensor_scalar(u[k][:, :], rows[k][:, 0:P], MASKED / 100, -100 * MASKED,
                                              ALU.is_lt, ALU.mult))
                    link(s, dve.tensor_tensor(v[k][:, :], u[k][:, :], rows[k][:, 0:P], ALU.add))
                    dve.wait_ge(logged, done(s))
                    link(s, dve.tensor_tensor(xn[k][:, :], v[k][:, :], w_[k][:, :], ALU.add))
                elif kind == "mix":
                    link(s, dve.scalar_tensor_tensor(u[k][:, :], rows[k][:, :], inv[k][:, 0:1], K.b3[:, :],
                                                     ALU.mult, ALU.add))
                    link(s, norm(s, v[k][:, :], u[k][:, :]))
                    link(s, dve.tensor_tensor(w_[k][:, :], v[k][:, :], K.gamma[:, :], ALU.mult))
                    link(s, dve.tensor_tensor(z[k][:, :], w_[k][:, :], K.beta[:, :], ALU.add))
                    link(s, dve.scalar_tensor_tensor(y[k][:, :], z[k][:, :], 0.0, x[k][:, :], ALU.max, ALU.add))
                if normed:
                    link(s, norm(s, xn[k][:, :], y[k][:, :]))
                per_seen.append(c[0])
                dve.sem_inc(fresh, 1)

            def make(s):
                dve.wait_ge(product, done(s))
                if scatters:
                    dve.wait_ge(s_sc[s.k], 16 * s.turn)
                dve.wait_ge(s_st[s.k], 16 * n_st * s.turn)
                if kind == "start":
                    for b in range(NPM):
                        a, e = b * B, min(cols, (b + 1) * B)
                        ins = dve.tensor_tensor(h[s.k][:, a:e], pm[b][:, 0:e - a], K.b0[:, a:e], ALU.add)
                elif kind == "max":
                    ins = dve.tensor_tensor(h[s.k][:, :], pm[0][:, 0:P], K.b1[:, :], ALU.add)
                elif kind == "sum":
                    ins = dve.tensor_copy(h[s.k][:, :], pm[0][:, 0:2 * P])
                else:
                    dve.tensor_copy(h[s.k][:, 0:P], pm[0][:, 0:P])
                    ins = dve.tensor_tensor(h[s.k][:, P:2 * P], pm[0][:, P:2 * P], K.bq[:, :], ALU.add)
                ins.then_inc(made, 1)
                if kind == "gat":
                    for b in range(0, wide, 2):
                        dve.wait_ge(wprod, s.n * wide + b + 1)
                        dve.tensor_copy(big[s.k][:, b * B:(b + 1) * B], pw[b % 4][:, :]).then_inc(wmade, 1)

            per_seen = []
            dve.sem_inc(fresh, CREDIT)
            if makes:
                dve.sem_inc(made, CREDIT)
            if kind == "start":
                dve.sem_inc(fresh, NTN)
                run(dve, NTN, R, [(make, 0)])
            elif makes:
                run(dve, NTN, R, [(finish, 0), (make, -1)])
            else:
                run(dve, NTN, R, [(finish, 0)])
            assert all(n == per for n in per_seen), (per, per_seen)

        @block.scalar
        def _(act):
            def root(s):
                for n in range(NORMS):
                    act.wait_ge(spread_v, s.n * NORMS + n + 1)
                    act.activation(sd[s.k][:, :], rsd[s.k][:, :], ACT.Sqrt).then_inc(spread_d, 1)

            def log(s):
                act.wait_ge(s_rows[s.k], 16 * (s.turn + 1))
                act.wait_ge(fresh, done(s, R))
                act.activation(w_[s.k][:, :], rows[s.k][:, P:2 * P], ACT.Ln).then_inc(logged, 1)

            def flip(s):
                act.wait_ge(turned, done(s))
                act.wait_ge(product, done(s, R))
                if kind == "gat" and (not isinstance(s.n, int) or s.n >= R):
                    act.wait_ge(wprod, wide * (s.n - 1))
                act.activation(xt[s.k][:, :], pt[s.k][:, 0:P], ACT.Copy).then_inc(flipped, 1)

            def wide_out(s):
                act.wait_ge(s_st[s.k], 16 * n_st * s.turn)
                for b in range(1, wide, 2):
                    act.wait_ge(wprod, s.n * wide + b + 1)
                    act.activation(big[s.k][:, b * B:(b + 1) * B], pw[b % 4][:, :], ACT.Copy).then_inc(wmade_a, 1)

            if makes:
                act.sem_inc(flipped, CREDIT)
            if kind == "lse":
                act.sem_inc(logged, CREDIT)
                run(act, NTN, R, [(log, 0)])
            elif kind == "start":
                run(act, NTN, R, [(flip, 0)])
            elif kind == "gat":
                run(act, NTN, R, [(root, 0), (wide_out, -1), (flip, 0)])
            elif makes:
                run(act, NTN, R, [(root, 0), (flip, 0)])
            else:
                run(act, NTN, R, [(root, 0)])


def four_layers(nc, io, n_nodes, n_edges):
    K = Kernel(nc, io, n_nodes, n_edges)
    with K.ctx:
        NP, EP = K.NP, K.EP
        make_constants(K)
        make_indices(K)
        table0 = K.dram("table0", (NP * RELS0, P))
        self0 = K.dram("self0", (NP, P))
        table = [K.dram(f"table{n}", (NP, P)) for n in (1, 2, 3)]
        table3 = K.dram("table_rel", (NP * RELS, P))
        x = [K.dram(f"x{n}", (NP, P)) for n in (1, 2, 3)]
        rows = K.dram("rows", (EP, P))
        rows2 = K.dram("rows2", (EP, 2 * P))
        scores = K.dram("scores", (K.NB * P, B))
        node_phase(K, "n0", "start", None, x_in=io["x"], self_out=self0, table=table0)
        edge_pass(K, "e0", "max", table0, K.idx0, rows)
        node_phase(K, "n1", "max", rows, x_in=io["x"], x_out=x[0], self_in=self0, table=table[0])
        edge_pass(K, "e1", "sum", table[0], io["src_t"], rows)
        node_phase(K, "n2", "sum", rows, x_in=x[0], x_out=x[1], table=table[1])
        edge_pass(K, "e2", "gat", table[1], io["src_t"], rows2)
        node_phase(K, "n3", "gat", rows2, x_in=x[1], x_out=x[2], table=table[2], table3=table3)
        edge_pass(K, "e3", "rel", table[2], io["src_t"], rows2, scores=scores)
        node_phase(K, "n4", "lse", rows2)
        edge_pass(K, "e4", "mix", table3, K.idx3, rows, scores=scores)
        node_phase(K, "n5", "mix", rows, x_in=x[2], x_out=io["out"])


def kernel(**inputs):
    import numpy as np
    import concourse.bacc as _bacc
    from concourse.bass_utils import run_bass_kernel_spmd as _run

    x = np.asarray(inputs["x"])
    nodes, edges = x.shape[0], inputs["src"].shape[0]
    n_nodes = -(-(nodes + 1) // (2 * P)) * 2 * P
    n_edges = -(-edges // (RING * B)) * RING * B

    def pad(a, n, value):
        a = np.asarray(a)
        return np.concatenate([a, np.full((n - a.shape[0], *a.shape[1:]), value, a.dtype)])

    def turned(a):
        return np.ascontiguousarray(a.reshape(-1, P).T)

    src, dst = pad(inputs["src"], n_edges, 0), pad(inputs["dst"], n_edges, nodes)
    rel32, rel8 = pad(inputs["edge_type_32"], n_edges, 0), pad(inputs["edge_type_8"], n_edges, 0)
    arrays = {
        "x": pad(x, n_nodes, 0), "src_t": turned(src), "dst_t": turned(dst), "rel8_t": turned(rel8),
        "rel32_t": turned(rel32), "rel32": rel32, "dst": np.concatenate([np.full(1, -1, dst.dtype), dst]),
    }
    names = {"w0": "L0_gnn_weight", "b0": "L0_gnn_bias", "w1": "L1_gnn_W", "b1": "L1_gnn_b", "w2": "L2_gnn_W",
             "attn_l": "L2_gnn_attn_l", "attn_r": "L2_gnn_attn_r", "b2": "L2_gnn_bias", "wr": "L3_gnn_W_r",
             "wq": "L3_gnn_Wq_w", "bq": "L3_gnn_Wq_b", "wk": "L3_gnn_Wk_w", "bk": "L3_gnn_Wk_b",
             "rule_emb": "L3_gnn_rule_emb", "b3": "L3_gnn_bias", "gamma": "L3_gnn_ln_gamma",
             "beta": "L3_gnn_ln_beta", "rule_ids": "L3_gnn_rule_ids"}
    arrays |= {short: np.ascontiguousarray(inputs[name]) for short, name in names.items()}
    nc = _bacc.Bacc("TRN2", target_bir_lowering=False, num_devices=1)
    io = {name: nc.dram_tensor(f"in_{name}", a.shape, mybir.dt.from_np(a.dtype), kind="ExternalInput").ap()
          for name, a in arrays.items()}
    io["out"] = nc.dram_tensor("out_x", (n_nodes, P), F32, kind="ExternalOutput").ap()
    four_layers(nc, io, n_nodes, n_edges)
    r = _run(nc, [{f"in_{name}": a for name, a in arrays.items()}], core_ids=[0])
    return r.results[0]["out_x"][0:nodes]
```

```python
from contextlib import ExitStack

import concourse.bass as bass
from concourse import mybir

ALU = mybir.AluOpType
ACT = mybir.ActivationFunctionType
F32 = mybir.dt.float32
BF16 = mybir.dt.bfloat16
I32 = mybir.dt.int32

P = 128
T = 4
B = T * P
RING = 4
HEADS = 4
RELS = 32
RELS_NODE = 8
RELS_EDGE = 4
RELS0 = 8
HUGE = 1.5e38
MASKED = -1e28
EPS = 1e-5
SLOPE = 0.2
CREDIT = 4


class Step:

    def __init__(self, i, k, ring):
        self.n, self.k, self.turn = i * ring + k, k % ring, i + k // ring
        self.prev = (k - 1) % ring


def done(s, back=0):
    return s.n + (CREDIT + 1 - back)


def run(eng, count, ring, stages):
    turns = count // ring

    def edge(steps):
        for m in steps:
            for stage, offset in stages:
                if 0 <= m + offset < count:
                    stage(Step(0, m + offset, ring))

    first = 1 + (min(offset for _, offset in stages) < 0)
    edge(range(-max(offset for _, offset in stages), first * ring))
    last = max(first, turns - 1)
    if last > first:
        with eng.Fori(first, last) as i:
            for k in range(ring):
                for stage, offset in stages:
                    stage(Step(i, k + offset, ring))
    edge(range(ring * last, count - min(offset for _, offset in stages)))


class Kernel:
    def __init__(self, nc, io, n_nodes, n_edges):
        self.nc, self.io = nc, io
        self.NTN = n_nodes // P
        self.NT = n_edges // P
        self.NB = n_edges // B
        self.NP, self.EP = n_nodes, n_edges
        self.ctx = ExitStack()
        self.sems = []

    def sem(self, ctx, name):
        self.sems.append(self.nc.alloc_semaphore(name))
        return self.sems[-1]

    def phase(self, ctx):
        nc = self.nc

        def clear():
            nc.all_engine_barrier()
            nc.clear_and_free_semaphores(self.sems)
            nc.all_engine_barrier()
            self.sems = []

        ctx.callback(clear)
        return ctx.enter_context(nc.Block())

    def sb(self, ctx, name, shape, dt=F32):
        return ctx.enter_context(self.nc.sbuf_tensor(name, shape, dt))

    def bank(self, ctx, name, shape=(P, B), dt=F32):
        return ctx.enter_context(self.nc.psum_tensor(name, list(shape), dt))

    def dram(self, name, shape, dt=F32):
        return self.nc.dram_tensor(name, shape, dt, kind="Internal").ap()


def make_constants(K):
    nc, io, sb = K.nc, K.io, K.sb
    c = K.ctx
    K.ident = sb(c, "ident", [P, P])
    K.ones = sb(c, "ones", [P, P])
    K.quarter = sb(c, "quarter", [P, P])
    K.upper = sb(c, "upper", [P, P])
    K.w0 = sb(c, "w0", [P, (RELS0 + 1) * P])
    K.b0 = sb(c, "b0", [P, (RELS0 + 1) * P])
    K.w1t = sb(c, "w1t", [P, P])
    K.b1 = sb(c, "b1", [P, P])
    K.w2 = sb(c, "w2", [P, 2 * P])
    K.left = sb(c, "left", [P, P])
    K.b2 = sb(c, "b2", [P, P])
    K.wr = sb(c, "wr", [P, RELS * P])
    K.wkq = sb(c, "wkq", [P, 2 * P])
    K.bq = sb(c, "bq", [P, P])
    K.rules = sb(c, "rules", [P, P])
    K.other = sb(c, "other", [RELS, P], BF16)
    K.filler = sb(c, "filler", [P, B])
    K.relid = sb(c, "relid", [RELS, 1])
    K.b3 = sb(c, "b3", [P, P])
    K.gamma = sb(c, "gamma", [P, P])
    K.beta = sb(c, "beta", [P, P])
    K.eps = sb(c, "eps", [P, 1])
    K.first_rows = K.dram("first_rows", (K.EP + K.NP, P))

    with ExitStack() as t:
        relid_i = sb(t, "relid_i", [RELS, 1], I32)
        right = sb(t, "right", [P, P])
        heads = sb(t, "heads", [P, P])
        al = sb(t, "al", [P, 1])
        ar = sb(t, "ar", [P, 1])
        w1 = sb(t, "w1", [P, P])
        w2t = sb(t, "w2t", [P, P])
        wk2 = sb(t, "wk2", [P, P])
        wk3 = sb(t, "wk3", [P, P])
        bk = sb(t, "bk", [P, 1])
        krel = sb(t, "krel", [P, RELS])
        hrel = sb(t, "hrel", [P, RELS])
        hrelm = sb(t, "hrelm", [P, RELS])
        ids = sb(t, "ids", [HEADS, 1], I32)
        emb = sb(t, "emb", [HEADS, P])
        embt = sb(t, "embt", [P, HEADS])
        vrule = sb(t, "vrule", [P, HEADS])
        pw1, pw2, pw2r = K.bank(t, "pw1"), K.bank(t, "pw2"), K.bank(t, "pw2r")
        pemb, pv, pk = K.bank(t, "pemb"), K.bank(t, "pv"), K.bank(t, "pk")
        loaded, ids_in, emb_in = (K.sem(t, n) for n in ("c_loaded", "c_ids", "c_emb"))
        made, turned, copied = (K.sem(t, n) for n in ("c_made", "c_turned", "c_copied"))
        products, chain, masks = K.sem(t, "c_products"), K.sem(t, "c_chain"), K.sem(t, "c_masks")
        LOADS = 18
        block = K.phase(t)

        @block.sync
        def _(sp):
            def load(dst, src):
                sp.dma_start(dst, src).then_inc(loaded, 16)

            load(K.w0[:, :].rearrange("i (r o) -> i r o", o=P), io["w0"].rearrange("r i o -> i r o"))
            load(K.b0[:, :], io["b0"].rearrange("r o -> (r o)").partition_broadcast(P))
            load(w1[:, :], io["w1"])
            load(K.b1[:, :], io["b1"].partition_broadcast(P))
            load(K.w2[:, 0:P], io["w2"])
            load(al[:, :], io["attn_l"].rearrange("h (f a) -> (h f) a", a=1))
            load(ar[:, :], io["attn_r"].rearrange("h (f a) -> (h f) a", a=1))
            load(K.b2[:, :], io["b2"].partition_broadcast(P))
            load(K.wr[:, :].rearrange("i (r o) -> i r o", o=P), io["wr"].rearrange("r i o -> i r o"))
            load(K.wkq[:, 0:P], io["wk"][0:P, :])
            load(K.wkq[:, P:2 * P], io["wq"])
            load(wk2[:, :], io["wk"][P:2 * P, :])
            load(wk3[:, :], io["wk"][2 * P:3 * P, :])
            load(K.bq[:, :], io["bq"].partition_broadcast(P))
            load(bk[:, :], io["bk"].rearrange("(f a) -> f a", a=1))
            load(K.b3[:, :], io["b3"].partition_broadcast(P))
            load(K.gamma[:, :], io["gamma"].partition_broadcast(P))
            load(K.beta[:, :], io["beta"].partition_broadcast(P))
            sp.dma_start(ids[:, :], io["rule_ids"].rearrange("(k a) -> k a", a=1)).then_inc(ids_in, 16)

        @block.gpsimd
        def _(pool):
            pool.memset(K.ident[:, :], 0.0).then_inc(masks, 1)
            pool.memset(K.upper[:, :], 1.0).then_inc(masks, 1)
            pool.memset(K.other[:, :], MASKED).then_inc(masks, 1)
            pool.iota(relid_i[:, :], [[0, 1]], base=0, channel_multiplier=1).then_inc(masks, 1)
            pool.wait_ge(masks, 4)
            pool.affine_select(out=K.ident[:, :], in_=K.ident[:, :], compare_op=ALU.not_equal, fill=1.0,
                               base=0, pattern=[[-1, P]], channel_multiplier=1).then_inc(masks, 1)
            pool.affine_select(out=K.upper[:, :], in_=K.upper[:, :], compare_op=ALU.is_ge, fill=0.0,
                               base=0, pattern=[[1, P]], channel_multiplier=-1).then_inc(masks, 1)
            pool.affine_select(out=K.other[:, :].rearrange("r (k q) -> r k q", q=RELS),
                               in_=K.other[:, :].rearrange("r (k q) -> r k q", q=RELS),
                               compare_op=ALU.not_equal, fill=0.0, base=0,
                               pattern=[[0, HEADS], [-1, RELS]], channel_multiplier=1).then_inc(masks, 1)
            pool.wait_ge(ids_in, 16)
            pool.indirect_dma_start(emb[:, :], None, io["rule_emb"],
                                    bass.IndirectOffsetOnAxis(ids[:, 0:1], 0)).then_inc(emb_in, 16)

        @block.vector
        def _(dve):
            dve.memset(K.filler[:, :], -HUGE)
            dve.memset(K.ones[:, :], 1.0)
            dve.memset(K.quarter[:, :], 1.0 / HEADS)
            dve.memset(K.eps[:, :], EPS)
            dve.memset(heads[:, :], 0.0).then_inc(chain, 1)
            dve.wait_ge(chain, 1)
            for h in range(HEADS):
                q = slice(32 * h, 32 * h + 32)
                ins = dve.memset(heads[q, q], 1.0)
            ins.then_inc(chain, 1)
            dve.wait_ge(chain, 2)
            dve.wait_ge(loaded, 16 * LOADS)
            dve.wait_ge(masks, 7)
            dve.tensor_copy(K.relid[:, :], relid_i[:, :])
            dve.tensor_scalar(K.left[:, :], heads[:, :], al[:, 0:1], None, ALU.mult)
            dve.tensor_scalar(right[:, :], heads[:, :], ar[:, 0:1], None, ALU.mult)
            dve.tensor_reduce(hrel[:, :], K.wr[:, :].rearrange("i (r o) -> i r o", o=P),
                              mybir.AxisListType.X, ALU.add).then_inc(chain, 1)
            dve.wait_ge(chain, 3)
            dve.tensor_scalar(hrelm[:, :], hrel[:, :], 1.0 / P, None, ALU.mult).then_inc(made, 1)
            dve.wait_ge(turned, 3)
            dve.tensor_copy(K.w1t[:, :], pw1[:, 0:P]).then_inc(copied, 1)
            dve.tensor_copy(w2t[:, :], pw2[:, 0:P]).then_inc(copied, 1)
            dve.tensor_copy(embt[:, :], pemb[:, 0:HEADS]).then_inc(copied, 1)
            dve.wait_ge(products, 3)
            dve.tensor_copy(K.w2[:, P:2 * P], pw2r[:, 0:P])
            dve.tensor_copy(vrule[:, :], pv[:, 0:HEADS]).then_inc(chain, 1)
            dve.tensor_scalar(krel[:, :], pk[:, 0:RELS], bk[:, 0:1], None, ALU.add).then_inc(chain, 1)
            dve.wait_ge(chain, 5)
            dve.tensor_tensor(K.rules[:, :].rearrange("f (k r) -> f k r", r=RELS),
                              vrule[:, :].unsqueeze(2).to_broadcast([P, HEADS, RELS]),
                              krel[:, :].unsqueeze(1).to_broadcast([P, HEADS, RELS]), ALU.add)

        @block.tensor
        def _(pe):
            pe.wait_ge(loaded, 16 * LOADS)
            pe.wait_ge(masks, 7)
            pe.wait_ge(emb_in, 16)
            pe.transpose(pw1[:, 0:P], w1[:, :], K.ident[:, :]).then_inc(turned, 1)
            pe.transpose(pw2[:, 0:P], K.w2[:, 0:P], K.ident[:, :]).then_inc(turned, 1)
            pe.transpose(pemb[:, 0:HEADS], emb[:, :], K.ident[0:HEADS, 0:HEADS]).then_inc(turned, 1)
            pe.wait_ge(copied, 3)
            pe.wait_ge(made, 1)
            pe.matmul(pw2r[:, 0:P], w2t[:, :], right[:, :], start=True, stop=True).then_inc(products, 1)
            pe.matmul(pv[:, 0:HEADS], wk3[:, :], embt[:, :], start=True, stop=True).then_inc(products, 1)
            pe.matmul(pk[:, 0:RELS], wk2[:, :], hrelm[:, :], start=True, stop=True).then_inc(products, 1)


def make_indices(K):
    nc, io, sb = K.nc, K.io, K.sb
    NT, NTN, EP = K.NT, K.NTN, K.EP
    K.idx0 = K.dram("idx0", (P, NT), I32)
    K.idx3 = K.dram("idx3", (P, NT), I32)
    K.keep = K.dram("keep", (EP,), BF16)
    K.cap = K.dram("cap", (EP,), BF16)
    K.rel = K.dram("rel", (EP,), BF16)
    K.hi, K.lo = sb(K.ctx, "hi", [P, NT], BF16), sb(K.ctx, "lo", [P, NT], BF16)
    K.iota = sb(K.ctx, "iota", [P, P], BF16)
    K.count = sb(K.ctx, "count", [P, NTN])
    with ExitStack() as t:
        src, rel8, rel32, rows0, rows3, cur, prev, flat32, dst, hi, lo = (
            sb(t, f"i_{n}", [P, NT], I32) for n in
            ("src", "rel8", "rel32", "rows0", "rows3", "cur", "prev", "flat32", "dst", "hi", "lo"))
        keep, cap, relb = (sb(t, f"i_{n}", [P, NT], BF16) for n in ("keep", "cap", "relb"))
        iota_i = sb(t, "iota_i", [P, P], I32)
        in_rows, in_marks, stored = K.sem(t, "i_in_rows"), K.sem(t, "i_in_marks"), K.sem(t, "i_stored")
        made, iotas, chain = K.sem(t, "i_made"), K.sem(t, "i_iotas"), K.sem(t, "i_chain")
        block = K.phase(t)

        @block.sync
        def _(sp):
            for a, b in ((src, io["src_t"]), (rel8, io["rel8_t"]), (rel32, io["rel32_t"]), (dst, io["dst_t"])):
                sp.dma_start(a[:, :], b).then_inc(in_rows, 16)
            for a, b in ((cur, io["dst"][1:EP + 1]), (prev, io["dst"][0:EP]), (flat32, io["rel32"])):
                sp.dma_start(a[:, :], b.rearrange("(p j) -> p j", p=P)).then_inc(in_marks, 16)
            sp.wait_ge(made, 1)
            sp.dma_start(K.idx0, rows0[:, :]).then_inc(stored, 16)
            sp.dma_start(K.idx3, rows3[:, :]).then_inc(stored, 16)
            sp.wait_ge(made, 2)
            for a, b in ((keep, K.keep), (cap, K.cap), (relb, K.rel)):
                sp.dma_start(b.rearrange("(p j) -> p j", p=P), a[:, :]).then_inc(stored, 16)
            sp.wait_ge(stored, 16 * 5)

        @block.gpsimd
        def _(pool):
            pool.iota(iota_i[:, :], [[1, P]], base=0, channel_multiplier=0).then_inc(iotas, 1)

        @block.vector
        def _(dve):
            dve.memset(K.count[:, :], 0.0)
            dve.wait_ge(in_rows, 16 * 4)
            dve.scalar_tensor_tensor(rows0[:, :], src[:, :], float(RELS0), rel8[:, :], ALU.mult, ALU.add)
            dve.scalar_tensor_tensor(rows3[:, :], src[:, :], float(RELS), rel32[:, :], ALU.mult,
                                     ALU.add).then_inc(made, 1)
            dve.tensor_scalar(hi[:, :], dst[:, :], 7, None, ALU.logical_shift_right)
            dve.tensor_scalar(lo[:, :], dst[:, :], P - 1, None, ALU.bitwise_and).then_inc(chain, 1)
            dve.wait_ge(in_marks, 16 * 3)
            dve.tensor_copy(relb[:, :], flat32[:, :])
            dve.tensor_tensor(keep[:, :], cur[:, :], prev[:, :], ALU.is_equal).then_inc(chain, 1)
            dve.wait_ge(chain, 1)
            dve.tensor_copy(K.hi[:, :], hi[:, :])
            dve.tensor_copy(K.lo[:, :], lo[:, :])
            dve.wait_ge(chain, 2)
            dve.tensor_scalar(cap[:, :], keep[:, :], 2 * HUGE, -HUGE, ALU.mult, ALU.add).then_inc(made, 1)
            dve.wait_ge(iotas, 1)
            dve.tensor_copy(K.iota[:, :], iota_i[:, :])


def make_bounds(K):
    nc, sb = K.nc, K.sb
    NTN = K.NTN
    K.node_idx = K.dram("node_idx", (NTN // T, P, T, 2), I32)
    K.node_inv = K.dram("node_inv", (NTN // T, P, T, 2))
    cnt = K.count
    with ExitStack() as t:
        names = ("tot", "running", "ones_n", "upto", "before", "end", "start", "has", "shift", "shift_if",
                 "least", "inverse", "node_f")
        tot, running, ones_n, upto, before, end, start, has, shift, shift_if, least, inverse, node_f = (
            sb(t, f"b_{n}", [P, NTN]) for n in names)
        node_i = sb(t, "b_node_i", [P, NTN], I32)
        nidx = sb(t, "b_nidx", [P, NTN, 2], I32)
        ninv = sb(t, "b_ninv", [P, NTN, 2])
        pin, ptot = K.bank(t, "pin"), K.bank(t, "ptot")
        prefix, chain, iotas = K.sem(t, "b_prefix"), K.sem(t, "b_chain"), K.sem(t, "b_iotas")
        made, stored = K.sem(t, "b_made"), K.sem(t, "b_stored")
        block = K.phase(t)

        @block.sync
        def _(sp):
            sp.wait_ge(made, 2)
            for a, b in ((nidx, K.node_idx), (ninv, K.node_inv)):
                sp.dma_start(b.rearrange("s p t a -> p s t a"),
                             a[:, :, :].rearrange("p (s t) a -> p s t a", t=T)).then_inc(stored, 16)
            sp.wait_ge(stored, 16 * 2)

        @block.gpsimd
        def _(pool):
            pool.iota(node_i[:, :], [[P, NTN]], base=K.EP, channel_multiplier=1).then_inc(iotas, 1)

        @block.tensor
        def _(pe):
            pe.matmul(pin[:, 0:NTN], K.upper[:, :], cnt[:, :], start=True, stop=True).then_inc(prefix, 1)
            pe.matmul(ptot[:, 0:NTN], K.ones[:, :], cnt[:, :], start=True, stop=True).then_inc(prefix, 1)

        @block.vector
        def _(dve):
            n = [0]

            def link(ins):
                n[0] += 1
                ins.then_inc(chain, 1)
                dve.wait_ge(chain, n[0])

            dve.wait_ge(iotas, 1)
            dve.tensor_copy(node_f[:, :], node_i[:, :])
            dve.memset(ones_n[:, :], 1.0)
            dve.wait_ge(prefix, 2)
            dve.tensor_copy(upto[:, :], pin[:, 0:NTN])
            link(dve.tensor_copy(tot[:, :], ptot[:, 0:NTN]))
            link(dve.tensor_tensor_scan(running[:, :], ones_n[:, :], tot[:, :], 0.0, ALU.mult, ALU.add))
            link(dve.tensor_tensor(before[:, :], running[:, :], tot[:, :], ALU.subtract))
            link(dve.tensor_tensor(end[:, :], upto[:, :], before[:, :], ALU.add))
            dve.tensor_scalar(nidx[:, :, 0], end[:, :], -1.0, 0.0, ALU.add, ALU.max)
            dve.tensor_tensor(start[:, :], end[:, :], cnt[:, :], ALU.subtract)
            dve.tensor_scalar(least[:, :], cnt[:, :], 1.0, None, ALU.max)
            link(dve.tensor_scalar(has[:, :], cnt[:, :], 1.0, None, ALU.min))
            dve.tensor_copy(ninv[:, :, 0], has[:, :])
            dve.reciprocal(inverse[:, :], least[:, :])
            link(dve.tensor_tensor(shift[:, :], start[:, :], node_f[:, :], ALU.subtract))
            link(dve.tensor_tensor(shift_if[:, :], shift[:, :], has[:, :], ALU.mult))
            dve.tensor_tensor(nidx[:, :, 1], shift_if[:, :], node_f[:, :], ALU.add).then_inc(made, 1)
            dve.tensor_tensor(ninv[:, :, 1], inverse[:, :], has[:, :], ALU.mult).then_inc(made, 1)


def hold(eng, carrier, sem, value):
    eng.wait_ge(sem, value)
    eng.sem_inc(carrier, 1)


def edge_pass(K, name, kind, table, idx, rows_out, scores=None, xt_in=None, table3=None):
    nc, sb, NB = K.nc, K.sb, K.NB
    fills = kind in ("gat", "rel", "mix")
    soft = kind in ("gat", "rel")
    W = 2 if soft else 1
    width = P + {"gat": HEADS, "rel": P}.get(kind, 0)
    with ExitStack() as t:
        S = lambda what: K.sem(t, f"{name}_{what}")

        def ring(what, shape=(P, B), dt=F32):
            return [sb(t, f"{name}_{what}{k}", list(shape), dt) for k in range(RING)]

        ix = ring("ix", (P, T), I32)
        g = ring("g", (P, T, P))
        o = ring("o")
        out = ring("out", (P, T, width))
        first = ring("first", (P, T, P)) if fills else None
        spread = ring("spread") if fills else None
        keep = ring("keepr", dt=BF16) if kind in ("sum", "mix") else None
        cap = ring("capr", dt=BF16) if kind != "sum" else None
        if soft:
            sc = sb(t, f"{name}_sc", [P, 1 + RING * B])
            mprev, d, grow, a, ss = (ring(x) for x in ("mprev", "d", "grow", "a", "ss"))
        if kind == "gat":
            gs, t2 = ring("gs"), ring("t2")
        if kind == "rel":
            relr = ring("relr", (RELS, B), BF16)
            hot = ring("hot", (RELS, B), BF16)
            xt, wide = ring("xt", (P, P)), ring("wide")
            prod = ring("prod")
        if kind == "mix":
            scr, d, a, at, am = (ring(x) for x in ("scr", "d", "a", "at", "am"))
        if kind == "max":
            onelo, onehi = ring("onelo", (P, T, P), BF16), ring("onehi", (P, T, K.NTN), BF16)
        NG = 4 if kind == "mix" else 2
        pg = [K.bank(t, f"{name}_pg{n}") for n in range(NG)]
        NF = 1 if kind == "rel" else 2
        pf = [K.bank(t, f"{name}_pf{n}") for n in range(NF)] if fills else None
        ps = [K.bank(t, f"{name}_ps{n}") for n in range(2 if kind == "gat" else 1)] if fills else None
        pw = [K.bank(t, f"{name}_pw{n}") for n in range(2)] if kind == "rel" else None
        pc = [K.bank(t, f"{name}_pc{n}") for n in range(2)] if kind == "max" else None
        NS = len(ps) if fills else 0
        po = [K.bank(t, f"{name}_po{n}") for n in range(W)]

        s_ix = [S(f"ix{k}") for k in range(RING)]
        s_in = [S(f"in{k}") for k in range(RING)]
        s_keep = [S(f"keep{k}") for k in range(RING)]
        s_g = [S(f"g{k}") for k in range(RING)]
        s_out = [S(f"out{k}") for k in range(RING)]
        s_sc = [S(f"sc{k}") for k in range(RING)] if kind == "rel" else None
        s_wide = [S(f"wide{k}") for k in range(RING)] if kind == "rel" else None
        s_clear = S("clear")
        onehot = S("onehot")
        counted = S("counted")
        added = S("added")
        projected = S("projected")
        wided = S("wided")
        turned = S("turned")
        turned_first = S("turned_first")
        scored = S("scored")
        back = S("back")
        filled = S("filled")
        hotted = S("hotted")
        prodded = S("prodded")
        sced = S("sced")
        maxed = S("maxed")
        diffed = S("diffed")
        relued_a = S("relued_a")
        weighed = S("weighed")
        summed = S("summed")
        scanned = S("scanned")
        copied = S("copied")
        scaled = S("scaled")
        relued = S("relued")
        grown = S("grown")
        exped = S("exped")
        evac = S("evac")
        n_in = (kind != "sum") + fills + (kind == "mix") + 2 * (kind == "rel")
        last = S("last")
        issued = S("issued")
        free = S("free")

        block = K.phase(t)
        at_edges = lambda ap, s: ap[bass.ds(s.n * B, B)]

        @block.sync
        def _(sp):
            def load_ix(s):
                hold(sp, free, s_g[s.k], 16 * T * s.turn)
                sp.dma_start(ix[s.k][:, :], idx[:, bass.ds(s.n * T, T)]).then_inc(s_ix[s.k], 16)

            def load_in(s):
                if fills:
                    hold(sp, free, turned_first, done(s, RING))
                    sp.dma_start(first[s.k][:, :, :], K.first_rows[bass.ds(s.n * B, B), :]
                                 .rearrange("(t p) f -> p t f", p=P)).then_inc(s_in[s.k], 16)
                if kind == "rel":
                    hold(sp, free, hotted, done(s, RING))
                    sp.dma_start(relr[s.k][:, :], at_edges(K.rel, s).partition_broadcast(RELS)).then_inc(s_in[s.k], 16)
                    hold(sp, free, projected, done(s, RING))
                    sp.dma_start(xt[s.k][:, :], xt_in[:, bass.ds(s.turn * P, P)]).then_inc(s_in[s.k], 16)
                if kind == "mix":
                    hold(sp, free, diffed, done(s, RING))
                    sp.dma_start(scr[s.k][:, :], scores[bass.ds(s.n * P, P), :]).then_inc(s_in[s.k], 16)
                if cap:
                    if fills:
                        hold(sp, free, filled, done(s, RING))
                    if kind != "mix":
                        hold(sp, free, maxed if soft else scanned, done(s, RING))
                    sp.dma_start(cap[s.k][:, :], at_edges(K.cap, s).partition_broadcast(P)).then_inc(s_in[s.k], 16)
                if keep:
                    hold(sp, free, scanned, done(s, RING))
                    sp.dma_start(keep[s.k][:, :], at_edges(K.keep, s).partition_broadcast(P)).then_inc(s_keep[s.k], 16)

            def clear(s):
                sp.dma_start(K.first_rows[bass.ds(s.n * B, B), :].rearrange("(p a) f -> p (a f)", p=P),
                             K.filler[:, :]).then_inc(s_clear, 16)

            run(sp, NB, RING, [(load_ix, 1), (load_in, 0)] + ([(clear, 0)] if kind == "sum" else []))
            if kind == "sum":
                sp.wait_ge(s_clear, 16 * NB)

        @block.gpsimd
        def _(pool):
            def gather(s):
                pool.wait_ge(s_ix[s.k], 16 * (s.turn + 1))
                pool.wait_ge(turned, done(s, RING))
                pool.sem_inc(issued, 1)
                for j in range(T):
                    pool.indirect_dma_start(g[s.k][:, j, :], None, table,
                                            bass.IndirectOffsetOnAxis(ix[s.k][:, j:j + 1], 0)).then_inc(s_g[s.k], 16)

            run(pool, NB, RING, [(gather, 0)])

        @block.tensor
        def _(pe):
            def turn(s):
                pe.wait_ge(s_g[s.k], 16 * T * (s.turn + 1))
                if kind in ("max", "sum"):
                    pe.wait_ge(scanned, done(s, NG))
                elif kind == "gat":
                    pe.wait_ge(copied, done(s, NG))
                elif kind == "rel":
                    pe.wait_ge(prodded, done(s, NG))
                else:
                    pe.wait_ge(weighed, done(s, NG))
                bank = pg[s.k % NG]
                for j in range(T):
                    ins = pe.transpose(bank[:, j * P:(j + 1) * P], g[s.k][:, j, :], K.ident[:, :])
                ins.then_inc(turned, 1)

            def turn_first(s):
                pe.wait_ge(s_in[s.k], 16 * n_in * (s.turn + 1))
                pe.wait_ge(filled, done(s, NF))
                for j in range(T):
                    ins = pe.transpose(pf[s.k % NF][:, j * P:(j + 1) * P], first[s.k][:, j, :], K.ident[:, :])
                ins.then_inc(turned_first, 1)

            def score(s):
                bank = ps[s.k % NS]
                if kind == "gat":
                    pe.wait_ge(sced, done(s, NS))
                    pe.wait_ge(scaled, done(s, NS))
                    pe.wait_ge(copied, done(s))
                    pe.wait_ge(filled, done(s))
                    pe.matmul(bank[:, :], K.left[:, :], gs[s.k][:, :], start=True, stop=False)
                    pe.matmul(bank[:, :], K.ident[:, :], spread[s.k][:, :], start=False, stop=True).then_inc(scored, 1)
                elif kind == "rel":
                    pe.wait_ge(sced, done(s, NS))
                    pe.wait_ge(prodded, done(s))
                    pe.wait_ge(hotted, done(s))
                    pe.matmul(bank[:, :], K.ones[:, :], prod[s.k][:, :], start=True, stop=False)
                    pe.matmul(bank[:, :], K.rules[:, :], spread[s.k][:, :], start=False, stop=False)
                    pe.matmul(bank[:, :], K.other[:, :], hot[s.k][:, :], start=False, stop=True).then_inc(scored, 1)
                else:
                    pe.wait_ge(copied, done(s, NS))
                    pe.wait_ge(exped, done(s))
                    pe.matmul(bank[:, :], K.quarter[:, :], a[s.k][:, :], start=True, stop=True).then_inc(scored, 1)

            def turn_back(s):
                pe.wait_ge(evac, done(s, 1))
                pe.wait_ge(weighed if kind == "rel" else scanned, done(s))
                for j in range(T):
                    ins = pe.transpose(po[0][:, j * P:(j + 1) * P], o[s.k][:, j * P:(j + 1) * P], K.ident[:, :])
                if soft:
                    pe.wait_ge(summed, done(s))
                    for j in range(T):
                        ins = pe.transpose(po[1][:, j * P:(j + 1) * P], ss[s.k][:, j * P:(j + 1) * P], K.ident[:, :])
                ins.then_inc(back, 1)

            def project(s):
                pe.wait_ge(s_in[s.k], 16 * n_in * (s.turn + 1))
                pe.wait_ge(wided, done(s, 2))
                at = (2 * RELS_NODE + RELS_EDGE * s.k) * P
                pe.matmul(pw[s.k % 2][:, :], xt[s.k][:, :], K.wr[:, at:at + B],
                          start=True, stop=True).then_inc(projected, 1)

            def count(s):
                pe.wait_ge(onehot, done(s))
                pe.wait_ge(added, done(s, 2))
                for j in range(T):
                    ins = pe.matmul(pc[s.k % 2][:, 0:K.NTN], onelo[s.k][:, j, :], onehi[s.k][:, j, :],
                                    start=(j == 0), stop=(j == T - 1))
                ins.then_inc(counted, 1)

            for x in (turned, turned_first, scored, back, counted, projected):
                pe.sem_inc(x, CREDIT)
            if kind == "gat":
                run(pe, NB, RING, [(turn_first, 2), (turn, 2), (turn_back, -2), (score, 2)])
            elif kind == "rel":
                run(pe, NB, RING, [(turn_first, 2), (turn, 2), (project, 0), (turn_back, -2), (score, 2)])
            elif kind == "mix":
                run(pe, NB, RING, [(turn, 2), (turn_first, 2), (score, 1), (turn_back, -1)])
            elif kind == "sum":
                run(pe, NB, RING, [(turn, 1), (turn_back, -1)])
            else:
                run(pe, NB, RING, [(turn, 1), (count, 0), (turn_back, -1)])

        @block.vector
        def _(dve):
            def one_hot(s):
                dve.wait_ge(s_in[s.k], 16 * n_in * (s.turn + 1))
                dve.wait_ge(scored, done(s, RING))
                dve.tensor_scalar(hot[s.k][:, :], relr[s.k][:, :], K.relid[:, 0:1], None,
                                  ALU.is_equal).then_inc(hotted, 1)

            def fill(s):
                dve.wait_ge(s_in[s.k], 16 * n_in * (s.turn + 1))
                dve.wait_ge(turned_first, done(s))
                dve.wait_ge(filled, done(s, 1))
                if kind != "mix":
                    dve.wait_ge(scored, done(s, RING))
                dve.tensor_tensor_scan(spread[s.k][:, :], cap[s.k][:, :], pf[s.k % NF][:, :],
                                       spread[s.prev][:, B - 1:B], ALU.min, ALU.max).then_inc(filled, 1)

            def key_query(s):
                dve.wait_ge(turned, done(s))
                dve.wait_ge(filled, done(s))
                dve.wait_ge(scored, done(s, RING))
                dve.tensor_tensor(prod[s.k][:, :], pg[s.k % 2][:, :], spread[s.k][:, :], ALU.mult).then_inc(prodded, 1)

            def here(s):
                return slice(1 + B * s.k, 1 + B * (s.k + 1))

            def leaky(s):
                dve.wait_ge(scaled, done(s))
                dve.tensor_tensor(sc[:, here(s)], ps[s.k % NS][:, :], t2[s.k][:, :], ALU.max).then_inc(sced, 1)

            def running_max(s):
                dve.wait_ge(sced, done(s))
                dve.wait_ge(maxed, done(s, 1))
                if s.k == 0:
                    dve.wait_ge(last, s.turn + 1)
                dve.tensor_tensor_scan(mprev[s.k][:, :], sc[:, B * s.k:B * (s.k + 1)], cap[s.k][:, :],
                                       mprev[s.prev][:, B - 1:B], ALU.max, ALU.min).then_inc(maxed, 1)
                if s.k == RING - 1:
                    dve.wait_ge(maxed, done(s, RING - 1))
                    dve.tensor_copy(sc[:, 0:1], sc[:, RING * B:RING * B + 1]).then_inc(last, 1)

            def difference(s):
                dve.wait_ge(maxed, done(s))
                dve.wait_ge(relued_a, done(s, RING))
                dve.tensor_tensor(d[s.k][:, :], sc[:, here(s)], mprev[s.k][:, :], ALU.subtract).then_inc(diffed, 1)

            def top(s):
                dve.wait_ge(back, done(s, RING))
                dve.tensor_tensor(o[s.k][:, :], sc[:, here(s)], mprev[s.k][:, :], ALU.max).then_inc(weighed, 1)

            def weigh(s):
                dve.wait_ge(exped, done(s))
                dve.tensor_tensor(gs[s.k][:, :], a[s.k][:, :], gs[s.k][:, :], ALU.mult).then_inc(weighed, 1)

            def sum_weights(s):
                dve.wait_ge(exped, done(s))
                dve.wait_ge(grown, done(s))
                dve.wait_ge(back, done(s, RING))
                dve.wait_ge(summed, done(s, 1))
                dve.tensor_tensor_scan(ss[s.k][:, :], grow[s.k][:, :], a[s.k][:, :],
                                       ss[s.prev][:, B - 1:B], ALU.mult, ALU.add).then_inc(summed, 1)

            def sum_rows(s):
                dve.wait_ge(grown, done(s))
                dve.wait_ge(weighed, done(s))
                dve.wait_ge(back, done(s, RING))
                dve.wait_ge(scanned, done(s, 1))
                dve.tensor_tensor_scan(o[s.k][:, :], grow[s.k][:, :], gs[s.k][:, :],
                                       o[s.prev][:, B - 1:B], ALU.mult, ALU.add).then_inc(scanned, 1)

            def one_hot_targets(s):
                dve.wait_ge(counted, done(s, RING))
                at = bass.ds(s.n * T, T)
                dve.tensor_tensor(onelo[s.k][:, :, :], K.iota[:, :].unsqueeze(1).to_broadcast([P, T, P]),
                                  K.lo[:, at].unsqueeze(2).to_broadcast([P, T, P]), ALU.is_equal)
                dve.tensor_tensor(onehi[s.k][:, :, :], K.iota[:, 0:K.NTN].unsqueeze(1).to_broadcast([P, T, K.NTN]),
                                  K.hi[:, at].unsqueeze(2).to_broadcast([P, T, K.NTN]),
                                  ALU.is_equal).then_inc(onehot, 1)

            def add_count(s):
                dve.wait_ge(counted, done(s))
                dve.wait_ge(added, done(s, 1))
                dve.tensor_tensor(K.count[:, :], K.count[:, :], pc[s.k % 2][:, 0:K.NTN], ALU.add).then_inc(added, 1)

            def scan_rows(s):
                dve.wait_ge(s_in[s.k] if kind == "max" else s_keep[s.k], 16 * (s.turn + 1))
                dve.wait_ge(turned, done(s))
                dve.wait_ge(back, done(s, RING))
                dve.wait_ge(scanned, done(s, 1))
                mark, op0, op1 = (cap, ALU.min, ALU.max) if kind == "max" else (keep, ALU.mult, ALU.add)
                dve.tensor_tensor_scan(o[s.k][:, :], mark[s.k][:, :], pg[s.k % NG][:, :],
                                       o[s.prev][:, B - 1:B], op0, op1).then_inc(scanned, 1)

            def attention(s):
                dve.wait_ge(filled, done(s))
                dve.wait_ge(exped, done(s, RING))
                dve.tensor_tensor(d[s.k][:, :], scr[s.k][:, :], spread[s.k][:, :], ALU.subtract).then_inc(diffed, 1)

            def mix_weigh(s):
                dve.wait_ge(copied, done(s))
                dve.wait_ge(turned, done(s))
                dve.tensor_tensor(am[s.k][:, :], pg[s.k % NG][:, :], at[s.k][:, :], ALU.mult).then_inc(weighed, 1)

            def mix_sum(s):
                dve.wait_ge(s_keep[s.k], 16 * (s.turn + 1))
                dve.wait_ge(weighed, done(s))
                dve.wait_ge(back, done(s, RING))
                dve.wait_ge(scanned, done(s, 1))
                dve.tensor_tensor_scan(o[s.k][:, :], keep[s.k][:, :], am[s.k][:, :],
                                       o[s.prev][:, B - 1:B], ALU.mult, ALU.add).then_inc(scanned, 1)

            for x, v in ((o, -HUGE if kind == "max" else 0.0), (spread, 0.0),
                         *(((mprev, -HUGE), (ss, 0.0)) if soft else ())):
                if x:
                    dve.memset(x[RING - 1][:, B - 1:B], v)
            if soft:
                dve.memset(sc[:, 0:1], 0.0)
            dve.memset(o[0][:, 0:1], 0.0).then_inc(last, 1)
            dve.wait_ge(last, 1)
            mine = [filled, hotted, prodded, maxed, diffed, weighed, summed, scanned, onehot, added]
            for x in mine + ([sced] if kind == "gat" else []):
                dve.sem_inc(x, CREDIT)
            if kind == "gat":
                run(dve, NB, RING, [(running_max, 0), (weigh, -1), (difference, 0), (sum_weights, -1), (fill, 2),
                                    (sum_rows, -1), (leaky, 1)])
            elif kind == "rel":
                run(dve, NB, RING, [(running_max, 0), (fill, 2), (difference, 0), (key_query, 2), (one_hot, 2),
                                    (sum_weights, -1), (top, 0)])
            elif kind == "mix":
                run(dve, NB, RING, [(fill, 2), (mix_weigh, 0), (attention, 2), (mix_sum, 0)])
            elif kind == "sum":
                run(dve, NB, RING, [(scan_rows, 0)])
            else:
                run(dve, NB, RING, [(scan_rows, 0), (one_hot_targets, 1), (add_count, -1)])

        @block.scalar
        def _(act):
            def copy_rows(s):
                act.wait_ge(turned, done(s))
                act.wait_ge(scored, done(s, RING))
                act.wait_ge(scanned, done(s, RING))
                act.activation(gs[s.k][:, :], pg[s.k % NG][:, :], ACT.Copy).then_inc(copied, 1)

            def scores_in(s):
                act.wait_ge(scored, done(s))
                if kind == "gat":
                    act.wait_ge(sced, done(s, RING))
                    act.activation(t2[s.k][:, :], ps[s.k % NS][:, :], ACT.Copy, scale=SLOPE).then_inc(scaled, 1)
                else:
                    act.wait_ge(diffed, done(s, RING))
                    act.wait_ge(maxed, done(s, RING - 1))
                    act.wait_ge(weighed, done(s, RING))
                    if s.k == RING - 1:
                        act.wait_ge(last, s.turn + 1)
                    act.wait_ge(s_sc[s.k], 16 * s.turn)
                    act.activation(sc[:, 1 + B * s.k:1 + B * (s.k + 1)], ps[s.k % NS][:, :], ACT.Copy,
                                   scale=float(P) ** -0.5).then_inc(sced, 1)

            def put_scores(s):
                act.wait_ge(sced, done(s))
                act.dma_start(scores[bass.ds(s.n * P, P), :],
                              sc[:, 1 + B * s.k:1 + B * (s.k + 1)]).then_inc(s_sc[s.k], 16)

            def exps(s):
                act.wait_ge(diffed, done(s))
                act.wait_ge(summed, done(s, RING))
                if kind == "gat":
                    act.wait_ge(scanned, done(s, RING))
                act.activation(grow[s.k][:, :], d[s.k][:, :], ACT.Relu).then_inc(relued, 1)
                act.activation(a[s.k][:, :], d[s.k][:, :], ACT.Relu, scale=-1.0).then_inc(relued_a, 1)
                act.wait_ge(relued, done(s))
                act.activation(grow[s.k][:, :], grow[s.k][:, :], ACT.Exp, scale=-1.0).then_inc(grown, 1)
                act.wait_ge(relued_a, done(s))
                act.activation(a[s.k][:, :], a[s.k][:, :], ACT.Exp, scale=-1.0).then_inc(exped, 1)

            def widen(s):
                act.wait_ge(s_wide[s.k], 16 * s.turn)
                act.wait_ge(projected, done(s))
                act.activation(wide[s.k][:, :], pw[s.k % 2][:, :], ACT.Copy).then_inc(wided, 1)

            def put_wide(s):
                act.wait_ge(wided, done(s))
                at = 2 * RELS_NODE + RELS_EDGE * s.k
                act.dma_start(table3.rearrange("(n r) f -> n r f", r=RELS)
                              [bass.ds(s.turn * P, P), at:at + RELS_EDGE, :],
                              wide[s.k][:, :].rearrange("p (r f) -> p r f", f=P)).then_inc(s_wide[s.k], 16)

            def exp_mix(s):
                act.wait_ge(diffed, done(s))
                act.wait_ge(scored, done(s, RING))
                act.activation(a[s.k][:, :], d[s.k][:, :], ACT.Exp).then_inc(exped, 1)

            def copy_mix(s):
                act.wait_ge(scored, done(s))
                act.wait_ge(weighed, done(s, RING))
                act.activation(at[s.k][:, :], ps[s.k % NS][:, :], ACT.Copy).then_inc(copied, 1)

            def store(s):
                act.wait_ge(back, done(s))
                act.wait_ge(s_out[s.k], 16 * s.turn)
                ins = act.activation(out[s.k][:, :, 0:P], po[0][:, :].rearrange("p (t f) -> p t f", f=P), ACT.Copy)
                if kind == "gat":
                    ins = act.activation(out[s.k][:, :, P:width],
                                         po[1][:, :].rearrange("p (t h f) -> p t h f", t=T, h=HEADS)[:, :, :, 0], ACT.Copy)
                elif kind == "rel":
                    ins = act.activation(out[s.k][:, :, P:width],
                                         po[1][:, :].rearrange("p (t f) -> p t f", f=P), ACT.Copy)
                ins.then_inc(evac, 1)

            def put(s):
                act.wait_ge(evac, done(s))
                act.dma_start(rows_out[bass.ds(s.n * B, B), :].rearrange("(t p) f -> p t f", p=P),
                              out[s.k][:, :, :]).then_inc(s_out[s.k], 16)

            for x in [copied, scaled, relued, relued_a, grown, exped, evac, wided] \
                    + ([] if kind == "gat" else [sced]):
                act.sem_inc(x, CREDIT)
            if kind == "gat":
                run(act, NB, RING, [(scores_in, 1), (copy_rows, 2), (exps, 0), (store, -2), (put, -3)])
            elif kind == "rel":
                run(act, NB, RING, [(scores_in, 1), (exps, 0), (put_scores, 0), (widen, 0), (store, -2), (put, -3),
                                    (put_wide, -1)])
            elif kind == "mix":
                run(act, NB, RING, [(exp_mix, 2), (copy_mix, 1), (store, -1), (put, -2)])
            else:
                run(act, NB, RING, [(store, -1), (put, -2)])
            for k in range(RING):
                act.wait_ge(s_out[k], 16 * (NB // RING))
                if kind == "rel":
                    act.wait_ge(s_sc[k], 16 * (NB // RING))
                    act.wait_ge(s_wide[k], 16 * (NB // RING))


def node_phase(K, name, kind, rows_in, x_in=None, x_out=None, self_in=None, self_out=None, table=None,
               xt_out=None, xt_in=None, table3=None):
    nc, sb = K.nc, K.sb
    N = K.NTN // T
    R = 4
    width = P + {"gat": HEADS, "lse": P}.get(kind, 0)
    scatters = kind in ("sum", "gat", "lse")
    gathers = kind != "start"
    makes = kind in ("start", "max", "sum", "gat")
    cols = {"start": (RELS0 + 1) * P, "max": P}.get(kind, 2 * P)
    first_rel = {"gat": 0, "lse": RELS_NODE}.get(kind)
    NORMS = {"max": 1, "sum": 1, "gat": 1, "mix": 2}.get(kind, 0)
    with ExitStack() as t:
        S = lambda what: K.sem(t, f"{name}_{what}")

        def ring(what, shape=(P, T, P), dt=F32):
            return [sb(t, f"{name}_{what}{k}", list(shape), dt) for k in range(R)]

        ids, inv = ring("ids", (P, T, 2), I32), ring("inv", (P, T, 2))
        x = ring("x") if kind != "lse" else None
        own = ring("own") if kind == "max" else None
        rows = ring("rows", (P, T, width)) if gathers else None
        steps = {"start": "", "max": "uy", "sum": "uy", "gat": "vwy", "lse": "uvw", "mix": "uvwzy"}[kind]
        u, v, w_, y, z = (ring(n) if n in steps else None for n in "uvwyz")
        recip = ring("recip", (P, T, HEADS)) if kind == "gat" else None
        xn = ring("xn") if gathers else None
        stats = ring("stats", (P, T, 6))
        mv = [ring(f"mv{n}_", (P, T, 2)) for n in range(2)]
        var, dev, rdev, shift = ([ring(f"{what}{n}_", (P, T)) for n in range(2)]
                                 for what in ("var", "dev", "rdev", "shift"))
        xt = ring("xt", (P, B)) if makes or table3 is not None else None
        wide = [sb(t, f"{name}_wide{j}", [P, RELS_NODE * P]) for j in range(T)] if table3 is not None else None
        pw = [K.bank(t, f"{name}_pw{n}") for n in range(2)] if table3 is not None else None
        s_wide = [S(f"wide{j}") for j in range(T)]
        projected, wided = S("projected"), S("wided")
        h = ring("h", (P, T, cols)) if makes else None
        pt = [K.bank(t, f"{name}_pt{k}") for k in range(2)]
        pm = [K.bank(t, f"{name}_pm{k}") for k in range(6 if kind == "start" else 4)] if makes else None
        s_ld = [S(f"ld{k}") for k in range(R)]
        s_rows = [S(f"rows{k}") for k in range(R)]
        s_sc = [S(f"sc{k}") for k in range(R)]
        s_st = [S(f"st{k}") for k in range(R)]
        n_ld = 2 * gathers + 1 + (kind == "max")
        n_st = {"start": 2, "max": 2, "sum": 2, "gat": 3, "lse": 0, "mix": 1}[kind]
        chains = {part: S(f"chain_{part}") for part in ("begin", "ready", "between", "end")}
        fresh = S("fresh")
        normed = S("normed")
        varied = [S(f"varied{n}") for n in range(2)]
        rooted = [S(f"rooted{n}") for n in range(2)]
        ready = [S(f"ready{n}") for n in range(2)]
        logged = S("logged")
        turned, flipped = S("turned"), S("flipped")
        product, made = S("product"), S("made")
        s_rest = S("rest")
        issued = S("issued")
        carried = S("carried")
        free = S("free")
        block = K.phase(t)
        result = x if kind == "start" else xn
        per_step = T if kind == "start" else 1

        def rows_of(ap, s):
            return ap[bass.ds(s.n * B, B), :].rearrange("(t p) f -> p t f", p=P)

        def tiles(s, back=0):
            return (s.n - back + 1 + CREDIT) * per_step

        def halves(s, back=0, j=T - 1, half=1):
            return 2 * (T * (s.n + (CREDIT - back)) + j) + half + 1

        def in_slot(k):
            return len(range(k, N, R))

        @block.sync
        def _(sp):
            def load(s):
                hold(sp, free, varied[NORMS - 1] if NORMS else fresh, done(s, R))
                if makes:
                    hold(sp, free, turned, done(s, R))
                if gathers:
                    hold(sp, free, s_rows[s.k], 16 * T * s.turn)
                    if scatters:
                        hold(sp, free, s_sc[s.k], 16 * T * s.turn)
                    sp.dma_start(ids[s.k][:, :, :], K.node_idx[bass.ds(s.n, 1), :, :, :]
                                 .rearrange("o p t a -> (o p) t a")).then_inc(s_ld[s.k], 16)
                    sp.dma_start(inv[s.k][:, :, :], K.node_inv[bass.ds(s.n, 1), :, :, :]
                                 .rearrange("o p t a -> (o p) t a")).then_inc(s_ld[s.k], 16)
                if kind == "lse":
                    hold(sp, free, projected, halves(s, R))
                    sp.dma_start(xt[s.k][:, :], xt_in[:, bass.ds(s.n * B, B)]).then_inc(s_ld[s.k], 16)
                else:
                    sp.dma_start(x[s.k][:, :, :], rows_of(x_in, s)).then_inc(s_ld[s.k], 16)
                if kind == "max":
                    sp.dma_start(own[s.k][:, :, :], rows_of(self_in, s)).then_inc(s_ld[s.k], 16)

            def store(s):
                if kind != "start":
                    hold(sp, free, fresh, done(s))
                    sp.dma_start(rows_of(x_out, s), xn[s.k][:, :, :]).then_inc(s_st[s.k], 16)
                if kind == "gat":
                    hold(sp, free, flipped, done(s))
                    sp.dma_start(xt_out[:, bass.ds(s.n * B, B)], xt[s.k][:, :]).then_inc(s_st[s.k], 16)
                if makes:
                    hold(sp, free, made, tiles(s))
                if kind == "start":
                    sp.dma_start(table[bass.ds(s.n * B * RELS0, B * RELS0), :]
                                 .rearrange("(t p r) f -> p t (r f)", p=P, r=RELS0),
                                 h[s.k][:, :, 0:RELS0 * P]).then_inc(s_st[s.k], 16)
                    sp.dma_start(rows_of(self_out, s), h[s.k][:, :, RELS0 * P:]).then_inc(s_st[s.k], 16)
                elif makes:
                    sp.dma_start(rows_of(table, s), h[s.k][:, :, 0:P]).then_inc(s_st[s.k], 16)

            if kind == "start":
                run(sp, N, R, [(load, 2), (store, -1)])
            else:
                run(sp, N, R, ([(store, -3 if kind == "mix" else -2)] if n_st else []) + [(load, 2)])
            if n_st:
                for k in range(R):
                    sp.wait_ge(s_st[k], 16 * n_st * in_slot(k))
            if kind == "gat":
                rest = [(n, r) for n in range(K.EP // RING // B, K.NTN) for r in range(2 * RELS_NODE, RELS, RELS_EDGE)]
                for n, r in rest:
                    sp.dma_start(table3.rearrange("(n r) f -> n r f", r=RELS)[n * P:(n + 1) * P, r:r + RELS_EDGE, :],
                                 K.filler[:, :].rearrange("p (r f) -> p r f", f=P)).then_inc(s_rest, 16)
                sp.wait_ge(s_rest, 16 * len(rest))

        @block.gpsimd
        def _(pool):
            def gather(s):
                pool.wait_ge(s_ld[s.k], 16 * n_ld * (s.turn + 1))
                pool.wait_ge(varied[0] if NORMS else fresh, done(s, R))
                pool.sem_inc(issued, 1)
                for j in range(T):
                    pool.indirect_dma_start(rows[s.k][:, j, :], None, rows_in,
                                            bass.IndirectOffsetOnAxis(ids[s.k][:, j, 0:1], 0)).then_inc(s_rows[s.k], 16)

            def scatter(s):
                if kind == "lse":
                    pool.wait_ge(fresh, done(s))
                else:
                    pool.wait_ge(made, done(s))
                pool.sem_inc(issued, 1)
                for j in range(T):
                    from_ = xn[s.k][:, j, :] if kind == "lse" else h[s.k][:, j, P:2 * P]
                    pool.indirect_dma_start(K.first_rows, bass.IndirectOffsetOnAxis(ids[s.k][:, j, 1:2], 0),
                                            from_, None).then_inc(s_sc[s.k], 16)

            if scatters:
                run(pool, N, R, [(gather, 1), (scatter, -1 if kind == "lse" else -2)])
                for k in range(R):
                    pool.wait_ge(s_sc[k], 16 * T * in_slot(k))
            elif gathers:
                run(pool, N, R, [(gather, 1)])

        @block.tensor
        def _(pe):
            def turn(s):
                if kind == "start":
                    pe.wait_ge(s_ld[s.k], 16 * n_ld * (s.turn + 1))
                else:
                    pe.wait_ge(fresh, done(s))
                pe.wait_ge(flipped, done(s, 2))
                for j in range(T):
                    ins = pe.transpose(pt[s.k % 2][:, j * P:(j + 1) * P], result[s.k][:, j, :], K.ident[:, :])
                ins.then_inc(turned, 1)

            def multiply(s):
                pe.wait_ge(flipped, done(s))
                w = {"start": K.w0, "max": K.w1t, "sum": K.w2, "gat": K.wkq}[kind]
                if kind != "start":
                    pe.wait_ge(made, done(s, 2))
                for j in range(T):
                    left = xt[s.k][:, j * P:(j + 1) * P]
                    if kind == "start":
                        pe.wait_ge(made, s.n * T + (j - 1 + CREDIT * T))
                        for c in range(0, cols, B):
                            ins = pe.matmul(pm[3 * (j % 2) + c // B][:, 0:min(B, cols - c)], left,
                                            w[:, c:min(cols, c + B)], start=True, stop=True)
                        ins.then_inc(product, 1)
                    else:
                        bank, at = pm[2 * (s.k % 2) + j // 2], (j % 2) * cols
                        ins = pe.matmul(bank[:, at:at + cols], left, w[:, 0:cols], start=True, stop=True)
                if kind != "start":
                    ins.then_inc(product, 1)

            def project(s):
                if kind == "lse":
                    pe.wait_ge(s_ld[s.k], 16 * n_ld * (s.turn + 1))
                else:
                    pe.wait_ge(flipped, done(s))
                for j in range(T):
                    for half in range(2):
                        pe.wait_ge(wided, halves(s, 0, j, half) - 2)
                        at = first_rel * P + half * B
                        pe.matmul(pw[half][:, :], xt[s.k][:, j * P:(j + 1) * P], K.wr[:, at:at + B],
                                  start=True, stop=True).then_inc(projected, 1)

            if table3 is not None:
                pe.sem_inc(projected, 2 * T * CREDIT)
            if makes:
                pe.sem_inc(turned, CREDIT)
                pe.sem_inc(product, CREDIT * per_step)
            if kind == "start":
                run(pe, N, R, [(turn, 0), (multiply, -1)])
            elif kind == "gat":
                run(pe, N, R, [(turn, -1), (multiply, -1), (project, -2)])
            elif kind == "lse":
                run(pe, N, R, [(project, 0)])
            elif makes:
                run(pe, N, R, [(turn, -1), (multiply, -1)])

        @block.vector
        def _(dve):
            per = {"begin": {"max": 2, "sum": 2, "gat": 4, "lse": 3, "mix": 1}.get(kind, 0) + 2 * bool(NORMS),
                   "ready": 1, "between": 5, "end": 1}
            links = {}

            def link(s, ins, part):
                links[part] += 1
                ins.then_inc(chains[part], 1)
                dve.wait_ge(chains[part], s.n * per[part] + links[part])

            def vary(s, n, in_, part):
                k = s.k
                for j in range(T):
                    ins = dve.bn_stats(stats[k][:, j, :], in_[:, j, :])
                link(s, ins, part)
                dve.sem_inc(carried, 1)
                for j in range(T):
                    ins = dve.bn_aggr(mv[n][k][:, j, :], stats[k][:, j, :])
                link(s, ins, part)
                dve.tensor_scalar(var[n][k][:, :], mv[n][k][:, :, 1], EPS, None, ALU.add).then_inc(varied[n], 1)

            def factors(s, n, part):
                k = s.k
                links[part] = 0
                dve.wait_ge(rooted[n], done(s))
                link(s, dve.reciprocal(rdev[n][k][:, :], dev[n][k][:, :]), part)
                dve.scalar_tensor_tensor(shift[n][k][:, :], mv[n][k][:, :, 0], -1.0, rdev[n][k][:, :],
                                         ALU.mult, ALU.mult).then_inc(ready[n], 1)

            def first_factors(s):
                factors(s, 0, "ready")

            def begin(s):
                k, each = s.k, range(T)
                links["begin"] = 0
                dve.wait_ge(s_rows[k], 16 * T * (s.turn + 1))
                dve.wait_ge(s_ld[k], 16 * n_ld * (s.turn + 1))
                if NORMS == 1:
                    dve.wait_ge(fresh, done(s, R))
                if kind == "max":
                    for j in each:
                        ins = dve.scalar_tensor_tensor(u[k][:, j, :], rows[k][:, j, :], inv[k][:, j, 0:1],
                                                       own[k][:, j, :], ALU.mult, ALU.add)
                    link(s, ins, "begin")
                    link(s, dve.scalar_tensor_tensor(y[k][:, :, :], u[k][:, :, :], 0.0, x[k][:, :, :],
                                                     ALU.max, ALU.add), "begin")
                elif kind == "sum":
                    for j in each:
                        ins = dve.tensor_scalar(u[k][:, j, :], rows[k][:, j, :], inv[k][:, j, 1:2], 0.0,
                                                ALU.mult, ALU.max)
                    link(s, ins, "begin")
                    link(s, dve.tensor_tensor(y[k][:, :, :], u[k][:, :, :], x[k][:, :, :], ALU.add), "begin")
                elif kind == "gat":
                    link(s, dve.reciprocal(recip[k][:, :, :], rows[k][:, :, P:width]), "begin")
                    for j in each:
                        ins = dve.tensor_tensor(v[k][:, j, :].rearrange("p (h f) -> p h f", h=HEADS),
                                                rows[k][:, j, 0:P].rearrange("p (h f) -> p h f", h=HEADS),
                                                recip[k][:, j, :].unsqueeze(2).to_broadcast([P, HEADS, P // HEADS]),
                                                ALU.mult)
                    link(s, ins, "begin")
                    for j in each:
                        ins = dve.scalar_tensor_tensor(w_[k][:, j, :], v[k][:, j, :], inv[k][:, j, 0:1],
                                                       K.b2[:, :], ALU.mult, ALU.add)
                    link(s, ins, "begin")
                    link(s, dve.tensor_tensor(y[k][:, :, :], w_[k][:, :, :], x[k][:, :, :], ALU.add), "begin")
                elif kind == "lse":
                    link(s, dve.tensor_scalar(u[k][:, :, :], rows[k][:, :, 0:P], MASKED / 100, -100 * MASKED,
                                              ALU.is_lt, ALU.mult), "begin")
                    link(s, dve.tensor_tensor(v[k][:, :, :], u[k][:, :, :], rows[k][:, :, 0:P], ALU.add), "begin")
                    dve.wait_ge(logged, done(s))
                    dve.wait_ge(s_sc[k], 16 * T * s.turn)
                    link(s, dve.tensor_tensor(xn[k][:, :, :], v[k][:, :, :], w_[k][:, :, :], ALU.add), "begin")
                    dve.sem_inc(fresh, 1)
                elif kind == "mix":
                    for j in each:
                        ins = dve.scalar_tensor_tensor(u[k][:, j, :], rows[k][:, j, :], inv[k][:, j, 0:1],
                                                       K.b3[:, :], ALU.mult, ALU.add)
                    link(s, ins, "begin")
                if NORMS:
                    vary(s, 0, u[k] if kind == "mix" else y[k], "begin")
                assert links["begin"] == per["begin"]

            def between(s):
                k = s.k
                links["between"] = 0
                dve.wait_ge(normed, done(s))
                dve.wait_ge(fresh, done(s, R))
                link(s, dve.tensor_tensor(w_[k][:, :, :], v[k][:, :, :],
                                          K.gamma[:, :].unsqueeze(1).to_broadcast([P, T, P]), ALU.mult), "between")
                link(s, dve.tensor_tensor(z[k][:, :, :], w_[k][:, :, :],
                                          K.beta[:, :].unsqueeze(1).to_broadcast([P, T, P]), ALU.add), "between")
                link(s, dve.scalar_tensor_tensor(y[k][:, :, :], z[k][:, :, :], 0.0, x[k][:, :, :],
                                                 ALU.max, ALU.add), "between")
                vary(s, 1, y[k], "between")
                assert links["between"] == per["between"]

            def end(s):
                factors(s, NORMS - 1, "end")
                if kind == "gat":
                    k = s.k
                    dve.wait_ge(turned, done(s, R))
                    dve.wait_ge(s_st[k], 16 * n_st * s.turn)
                    for j in range(T):
                        ins = dve.tensor_scalar(xn[k][:, j, :], y[k][:, j, :], mv[0][k][:, j, 0:1],
                                                rdev[0][k][:, j:j + 1], ALU.subtract, ALU.mult)
                    ins.then_inc(fresh, 1)

            def make(s):
                if scatters:
                    dve.wait_ge(s_sc[s.k], 16 * T * s.turn)
                dve.wait_ge(s_st[s.k], 16 * n_st * s.turn)
                if kind == "start":
                    for j in range(T):
                        dve.wait_ge(product, s.n * T + (j + 1 + CREDIT * T))
                        for c in range(0, cols, B):
                            e = min(cols, c + B)
                            ins = dve.tensor_tensor(h[s.k][:, j, c:e], pm[3 * (j % 2) + c // B][:, 0:e - c],
                                                    K.b0[:, c:e], ALU.add)
                        ins.then_inc(made, 1)
                    return
                dve.wait_ge(product, done(s))
                for q in range(2):
                    bank = pm[2 * (s.k % 2) + q][:, 0:2 * cols].rearrange("p (t c) -> p t c", t=2)
                    here = h[s.k][:, 2 * q:2 * q + 2, :]
                    if kind == "max":
                        ins = dve.tensor_tensor(here, bank, K.b1[:, :].unsqueeze(1).to_broadcast([P, 2, P]), ALU.add)
                    elif kind == "sum":
                        ins = dve.tensor_copy(here, bank)
                    else:
                        dve.tensor_copy(here[:, :, 0:P], bank[:, :, 0:P])
                        ins = dve.tensor_tensor(here[:, :, P:2 * P], bank[:, :, P:2 * P],
                                                K.bq[:, :].unsqueeze(1).to_broadcast([P, 2, P]), ALU.add)
                ins.then_inc(made, 1)

            if makes:
                dve.sem_inc(made, CREDIT * per_step)
            for q in ready + varied:
                dve.sem_inc(q, CREDIT)
            if not NORMS or kind == "gat":
                dve.sem_inc(fresh, CREDIT + (N if kind == "start" else 0))
            if kind == "start":
                run(dve, N, R, [(make, 0)])
            elif kind == "lse":
                run(dve, N, R, [(begin, 0)])
            elif kind == "mix":
                run(dve, N, R, [(end, -3), (first_factors, -1), (between, -2), (begin, 0)])
            else:
                run(dve, N, R, [(end, -1), (make, -2), (begin, 0)])

        @block.scalar
        def _(act):
            def root(s, n=0):
                act.wait_ge(varied[n], done(s))
                act.activation(dev[n][s.k][:, :], var[n][s.k][:, :], ACT.Sqrt).then_inc(rooted[n], 1)

            def root_again(s):
                root(s, 1)

            def normalize(s, n, out, in_, signal):
                act.wait_ge(ready[n], done(s))
                for j in range(T):
                    ins = act.activation(out[:, j, :], in_[:, j, :], ACT.Identity,
                                         bias=shift[n][s.k][:, j:j + 1], scale=rdev[n][s.k][:, j:j + 1])
                ins.then_inc(signal, 1)

            def norm_layer(s):
                normalize(s, 0, v[s.k], u[s.k], normed)

            def norm_x(s):
                if makes:
                    act.wait_ge(turned, done(s, R))
                act.wait_ge(s_st[s.k], 16 * n_st * s.turn)
                normalize(s, NORMS - 1, xn[s.k], y[s.k], fresh)

            def log(s):
                act.wait_ge(s_rows[s.k], 16 * T * (s.turn + 1))
                act.wait_ge(fresh, done(s, R))
                act.activation(w_[s.k][:, :, :], rows[s.k][:, :, P:2 * P], ACT.Ln).then_inc(logged, 1)

            def flip(s):
                act.wait_ge(turned, done(s))
                act.wait_ge(product, tiles(s, R))
                if kind == "gat":
                    act.wait_ge(s_st[s.k], 16 * n_st * s.turn)
                    act.wait_ge(projected, halves(s, R))
                act.activation(xt[s.k][:, :], pt[s.k % 2][:, :], ACT.Copy).then_inc(flipped, 1)

            def widen(s):
                for j in range(T):
                    act.wait_ge(s_wide[j], 16 * s.n)
                    for half in range(2):
                        act.wait_ge(projected, halves(s, 0, j, half))
                        act.activation(wide[j][:, half * B:(half + 1) * B], pw[half][:, :], ACT.Copy).then_inc(wided, 1)
                    if j:
                        put_wide(s, j - 1)
                put_wide(s, T - 1)

            def put_wide(s, j):
                act.wait_ge(wided, halves(s, 0, j))
                act.dma_start(table3.rearrange("(n r) f -> n r f", r=RELS)
                              [bass.ds(s.n * B + j * P, P), first_rel:first_rel + RELS_NODE, :],
                              wide[j][:, :].rearrange("p (r f) -> p r f", f=P)).then_inc(s_wide[j], 16)

            if makes:
                act.sem_inc(flipped, CREDIT)
            for q in rooted + [normed] + ([fresh] if NORMS and kind != "gat" else []):
                act.sem_inc(q, CREDIT)
            if table3 is not None:
                act.sem_inc(wided, 2 * T * CREDIT)
            if kind == "lse":
                act.sem_inc(logged, CREDIT)
                run(act, N, R, [(log, 0), (widen, -1)])
            elif kind == "gat":
                run(act, N, R, [(flip, -1), (root, 0), (widen, -2)])
            elif kind == "start":
                run(act, N, R, [(flip, 0)])
            elif makes:
                run(act, N, R, [(norm_x, -1), (flip, -1), (root, 0)])
            else:
                run(act, N, R, [(norm_x, -3), (norm_layer, -1), (root_again, -2), (root, 0)])
            if table3 is not None:
                for j in range(T):
                    act.wait_ge(s_wide[j], 16 * N)


def four_layers(nc, io, n_nodes, n_edges, nodes):
    K = Kernel(nc, io, n_nodes, n_edges)
    with K.ctx:
        NP, EP = K.NP, K.EP
        make_constants(K)
        assert NP >= EP // RING // B * P >= nodes
        table0 = K.dram("table0", (NP * RELS0, P))
        self0 = K.dram("self0", (NP, P))
        table = [K.dram(f"table{n}", (NP, P)) for n in (1, 2, 3)]
        table3 = K.dram("table_rel", (NP * RELS, P))
        x = [K.dram(f"x{n}", (NP, P)) for n in (1, 2, 3)]
        xt3 = K.dram("xt3", (P, NP))
        rows = K.dram("rows", (EP, P))
        rows_gat = K.dram("rows_gat", (EP, P + HEADS))
        rows_rel = K.dram("rows_rel", (EP, 2 * P))
        scores = K.dram("scores", (K.NB * P, B))
        make_indices(K)
        node_phase(K, "n0", "start", None, x_in=io["x"], self_out=self0, table=table0)
        edge_pass(K, "e0", "max", table0, K.idx0, rows)
        make_bounds(K)
        node_phase(K, "n1", "max", rows, x_in=io["x"], x_out=x[0], self_in=self0, table=table[0])
        edge_pass(K, "e1", "sum", table[0], io["src_t"], rows)
        node_phase(K, "n2", "sum", rows, x_in=x[0], x_out=x[1], table=table[1])
        edge_pass(K, "e2", "gat", table[1], io["src_t"], rows_gat)
        node_phase(K, "n3", "gat", rows_gat, x_in=x[1], x_out=x[2], table=table[2], xt_out=xt3,
                   table3=table3)
        edge_pass(K, "e3", "rel", table[2], io["src_t"], rows_rel, scores=scores, xt_in=xt3, table3=table3)
        node_phase(K, "n4", "lse", rows_rel, xt_in=xt3, table3=table3)
        edge_pass(K, "e4", "mix", table3, K.idx3, rows, scores=scores)
        node_phase(K, "n5", "mix", rows, x_in=x[2], x_out=io["out"])


def kernel(**inputs):
    import numpy as np
    import concourse.bacc as _bacc
    from concourse.bass_utils import run_bass_kernel_spmd as _run

    x = np.asarray(inputs["x"])
    nodes, edges = x.shape[0], inputs["src"].shape[0]
    n_nodes = -(-(nodes + 1) // B) * B
    n_edges = -(-edges // (RING * B)) * RING * B

    def pad(a, n, value):
        a = np.asarray(a)
        return np.concatenate([a, np.full((n - a.shape[0], *a.shape[1:]), value, a.dtype)])

    def turned(a):
        return np.ascontiguousarray(a.reshape(-1, P).T)

    src, dst = pad(inputs["src"], n_edges, 0), pad(inputs["dst"], n_edges, nodes)
    rel32, rel8 = pad(inputs["edge_type_32"], n_edges, 0), pad(inputs["edge_type_8"], n_edges, 0)
    arrays = {
        "x": pad(x, n_nodes, 0), "src_t": turned(src), "dst_t": turned(dst), "rel8_t": turned(rel8),
        "rel32_t": turned(rel32), "rel32": rel32, "dst": np.concatenate([np.full(1, -1, dst.dtype), dst]),
    }
    names = {"w0": "L0_gnn_weight", "b0": "L0_gnn_bias", "w1": "L1_gnn_W", "b1": "L1_gnn_b", "w2": "L2_gnn_W",
             "attn_l": "L2_gnn_attn_l", "attn_r": "L2_gnn_attn_r", "b2": "L2_gnn_bias", "wr": "L3_gnn_W_r",
             "wq": "L3_gnn_Wq_w", "bq": "L3_gnn_Wq_b", "wk": "L3_gnn_Wk_w", "bk": "L3_gnn_Wk_b",
             "rule_emb": "L3_gnn_rule_emb", "b3": "L3_gnn_bias", "gamma": "L3_gnn_ln_gamma",
             "beta": "L3_gnn_ln_beta", "rule_ids": "L3_gnn_rule_ids"}
    arrays |= {short: np.ascontiguousarray(inputs[name]) for short, name in names.items()}
    nc = _bacc.Bacc("TRN2", target_bir_lowering=False, num_devices=1)
    io = {name: nc.dram_tensor(f"in_{name}", a.shape, mybir.dt.from_np(a.dtype), kind="ExternalInput").ap()
          for name, a in arrays.items()}
    io["out"] = nc.dram_tensor("out_x", (n_nodes, P), F32, kind="ExternalOutput").ap()
    four_layers(nc, io, n_nodes, n_edges, nodes)
    r = _run(nc, [{f"in_{name}": a for name, a in arrays.items()}], core_ids=[0])
    return r.results[0]["out_x"][0:nodes]
```
